# Optimizing a Trainium2 kernel written in Bass

```python
import numpy as np
import jax
import jax.numpy as jnp

def _softmax(x, axis=-1):
    return jax.nn.softmax(x, axis=axis)

def _gelu(x):
    return jax.nn.gelu(x, approximate=True)

def _silu(x):
    return jax.nn.silu(x)

def _sigmoid(x):
    return jax.nn.sigmoid(x)

def _layernorm(x, axis=-1, eps=1e-05):
    m = jnp.mean(x, axis=axis, keepdims=True)
    v = jnp.var(x, axis=axis, keepdims=True)
    return (x - m) / jnp.sqrt(v + eps)

def _scatter_add(tgt, idx, src, axis=0):
    return tgt.at[idx].add(src)

def _segment_sum(src, seg, n):
    return jax.ops.segment_sum(src, seg, n)
kernel_name = 'mk_sandwich_d1_jaxref_r8_72153a'

def setup_inputs(seed: int=0):
    np.random.seed(seed)
    _w = jnp.asarray

    def _L0_attn_setup():
        import jax, jax.numpy as jnp
        import numpy as np
        D_MODEL, N_HEADS, N_KV, HEAD_DIM, D_LAT = (128, 8, 2, 128, 32)
        N_REP = N_HEADS // N_KV
        B, T = (2, 256)
        key = jax.random.key(seed)
        ks = jax.random.split(key, 8)
        s = lambda fan_in: 1.0 / np.sqrt(fan_in)
        return {'x': jax.random.normal(ks[0], (B, T, D_MODEL), jnp.float32), 'wq': jax.random.normal(ks[1], (D_MODEL, N_HEADS * HEAD_DIM), jnp.float32) * s(D_MODEL), 'wk_down': jax.random.normal(ks[2], (D_MODEL, N_KV * D_LAT), jnp.float32) * s(D_MODEL), 'wv_down': jax.random.normal(ks[3], (D_MODEL, N_KV * D_LAT), jnp.float32) * s(D_MODEL), 'wk_up': jax.random.normal(ks[4], (D_LAT, HEAD_DIM), jnp.float32) * s(D_LAT), 'wv_up': jax.random.normal(ks[5], (D_LAT, HEAD_DIM), jnp.float32) * s(D_LAT), 'wo': jax.random.normal(ks[6], (N_HEADS * HEAD_DIM, D_MODEL), jnp.float32) * s(N_HEADS * HEAD_DIM)}
    _L0_attn_in = _L0_attn_setup()

    def _L0_ffn_setup():
        import jax, jax.numpy as jnp
        import numpy as np
        D_IN, D_HID = (128, 512)

        def _ternary(key, shape):
            return jax.random.randint(key, shape, -1, 2).astype(jnp.float32)

        def _tlin(x, w, s):
            return jnp.einsum('bsi,oi->bso', x, w) * s
        key = jax.random.key(seed)
        ks = jax.random.split(key, 12)
        inv = lambda fan: 1.0 / np.sqrt(fan).astype(np.float32)
        return {'x': jax.random.normal(ks[0], (4, 256, D_IN), dtype=jnp.float32), 'w1_w': _ternary(ks[1], (D_HID, D_IN)), 'w1_s': jax.random.uniform(ks[2], (D_HID,), dtype=jnp.float32) * inv(D_IN), 'w2_w': _ternary(ks[3], (D_HID, D_IN)), 'w2_s': jax.random.uniform(ks[4], (D_HID,), dtype=jnp.float32) * inv(D_IN), 'h1_w': _ternary(ks[5], (D_HID, D_HID)), 'h1_s': jax.random.uniform(ks[6], (D_HID,), dtype=jnp.float32) * inv(D_HID), 'h2_w': _ternary(ks[7], (D_HID, D_HID)), 'h2_s': jax.random.uniform(ks[8], (D_HID,), dtype=jnp.float32) * inv(D_HID), 'w3_w': _ternary(ks[9], (D_IN, D_HID)), 'w3_s': jax.random.uniform(ks[10], (D_IN,), dtype=jnp.float32) * inv(D_HID)}
    _L0_ffn_in = _L0_ffn_setup()
    _d = {'L0_attn_x': _L0_attn_in['x'], 'L0_attn_wq': _L0_attn_in['wq'], 'L0_attn_wk_down': _L0_attn_in['wk_down'], 'L0_attn_wv_down': _L0_attn_in['wv_down'], 'L0_attn_wk_up': _L0_attn_in['wk_up'], 'L0_attn_wv_up': _L0_attn_in['wv_up'], 'L0_attn_wo': _L0_attn_in['wo'], 'L0_ffn_w1_w': _L0_ffn_in['w1_w'], 'L0_ffn_w1_s': _L0_ffn_in['w1_s'], 'L0_ffn_w2_w': _L0_ffn_in['w2_w'], 'L0_ffn_w2_s': _L0_ffn_in['w2_s'], 'L0_ffn_h1_w': _L0_ffn_in['h1_w'], 'L0_ffn_h1_s': _L0_ffn_in['h1_s'], 'L0_ffn_h2_w': _L0_ffn_in['h2_w'], 'L0_ffn_h2_s': _L0_ffn_in['h2_s'], 'L0_ffn_w3_w': _L0_ffn_in['w3_w'], 'L0_ffn_w3_s': _L0_ffn_in['w3_s']}
    _x0 = _d['L0_attn_x']
    _d['L0_attn_x'] = jax.random.normal(jax.random.fold_in(jax.random.key(seed), 1), (2, 2048, 128), dtype=_x0.dtype)
    del _x0
    return _d

def reference(L0_attn_x, L0_attn_wq, L0_attn_wk_down, L0_attn_wv_down, L0_attn_wk_up, L0_attn_wv_up, L0_attn_wo, L0_ffn_w1_w, L0_ffn_w1_s, L0_ffn_w2_w, L0_ffn_w2_s, L0_ffn_h1_w, L0_ffn_h1_s, L0_ffn_h2_w, L0_ffn_h2_s, L0_ffn_w3_w, L0_ffn_w3_s):

    def _L0_attn_ref(x, wq, wk_down, wv_down, wk_up, wv_up, wo):
        import jax, jax.numpy as jnp
        import numpy as np
        D_MODEL, N_HEADS, N_KV, HEAD_DIM, D_LAT = (128, 8, 2, 128, 32)
        N_REP = N_HEADS // N_KV
        B, T = (2, 256)
        Bq, Tq, _ = x.shape
        scale = HEAD_DIM ** (-0.5)
        q = (x @ wq).reshape(Bq, Tq, N_KV, N_REP, HEAD_DIM)
        k_lat = (x @ wk_down).reshape(Bq, Tq, N_KV, D_LAT)
        v_lat = (x @ wv_down).reshape(Bq, Tq, N_KV, D_LAT)
        k = jnp.einsum('bkhl,ld->bkhd', k_lat, wk_up)
        v = jnp.einsum('bkhl,ld->bkhd', v_lat, wv_up)
        scores = jnp.einsum('bqhrd,bkhd->bhrqk', q, k) * scale
        causal = jnp.tril(jnp.ones((Tq, Tq), dtype=bool))
        scores = jnp.where(causal, scores, jnp.finfo(scores.dtype).min)
        probs = jax.nn.softmax(scores, axis=-1)
        y = jnp.einsum('bhrqk,bkhd->bqhrd', probs, v)
        y = y.reshape(Bq, Tq, N_HEADS * HEAD_DIM)
        return y @ wo

    def _L0_ffn_ref(x, w1_w, w1_s, w2_w, w2_s, h1_w, h1_s, h2_w, h2_s, w3_w, w3_s):
        import jax, jax.numpy as jnp
        import numpy as np
        D_IN, D_HID = (128, 512)

        def _ternary(key, shape):
            return jax.random.randint(key, shape, -1, 2).astype(jnp.float32)

        def _tlin(x, w, s):
            return jnp.einsum('bsi,oi->bso', x, w) * s
        h = jax.nn.silu(_tlin(x, w1_w, w1_s)) * _tlin(x, w2_w, w2_s)
        h = jax.nn.gelu(_tlin(h, h1_w, h1_s), approximate=False)
        h = jax.nn.gelu(_tlin(h, h2_w, h2_s), approximate=False)
        return _tlin(h, w3_w, w3_s)
    x = L0_attn_x
    x = x + _layernorm(_L0_attn_ref(_layernorm(x, axis=-1), L0_attn_wq, L0_attn_wk_down, L0_attn_wv_down, L0_attn_wk_up, L0_attn_wv_up, L0_attn_wo), axis=-1)
    x = x + _layernorm(_L0_ffn_ref(_layernorm(x, axis=-1), L0_ffn_w1_w, L0_ffn_w1_s, L0_ffn_w2_w, L0_ffn_w2_s, L0_ffn_h1_w, L0_ffn_h1_s, L0_ffn_h2_w, L0_ffn_h2_s, L0_ffn_w3_w, L0_ffn_w3_s), axis=-1)
    return x

_drawn_inputs = setup_inputs


def setup_inputs(seed=0):
    import zlib

    import numpy as np

    out = dict(_drawn_inputs(seed))
    spreads = {}
    factors = {}
    for name, (base, spread) in spreads.items():
        noise = np.random.default_rng([zlib.crc32(name.encode()), seed]).standard_normal(out[name].shape)
        drawn = base * np.exp(spread * noise) if base else spread * noise
        out[name] = jnp.asarray(drawn.astype(out[name].dtype))
    for name, factor in factors.items():
        out[name] = (out[name] * factor).astype(out[name].dtype)
    return out
```

```python
import numpy as np
import concourse.bass as bass
from concourse import mybir
from contextlib import ExitStack

F32 = mybir.dt.float32
F32R = mybir.dt.float32r
BF16 = mybir.dt.bfloat16
F16 = mybir.dt.float16
ALU = mybir.AluOpType
ACT = mybir.ActivationFunctionType
AX = mybir.AxisListType
ds = bass.ds

P = 128
BATCH, SEQ, DM = 2, 2048, 128
TOK = BATCH * SEQ
HEADS, KV, HD, LAT = 8, 2, 128, 32
REP = HEADS // KV
HID = 512
EPS = 1e-5
GT = 512
TPG = GT // P
GROUPS = TOK // GT
QG = SEQ // GT
KT = SEQ // P
VW = LAT + 1
VPARTS = 3
VC = VPARTS * VW
SROWS = 3 * LAT
SCALE = float(HD) ** -0.5
NEG = -1e30
PSHIFT = 14.0 * float(np.log(2.0))


STORES = 2 * KV + 3


class Chain:

    def __init__(self, eng, sem, base=0):
        self.eng, self.sem, self.base, self.n = eng, sem, base, 0

    def __call__(self, ins):
        self.n += 1
        ins.then_inc(self.sem, 1)
        self.eng.wait_ge(self.sem, self.base + self.n)


def layer(nc, x, wqT, wkd, wvd, wkuT, wvuT, wo, w1T, w2T, h1T, h2T, w3T, s1, s2, sh1, sh2, s3, out):
    q_dram = nc.dram_tensor("q_parts", [2, HEADS * LAT, TOK], F32, kind="Internal").ap()
    k_dram = nc.dram_tensor("k_parts", [2, KV * LAT, TOK], F32, kind="Internal").ap()
    v_dram = nc.dram_tensor("v_parts", [P, KV, TOK // P, VC], BF16, kind="Internal").ap()
    with ExitStack() as keep:
        sb = lambda name, shape, dt: keep.enter_context(nc.sbuf_tensor(name, shape, dt))
        W = {}
        W["ident"] = sb("ident", [P, P], F32)
        W["identb"] = sb("identb", [P, P], BF16)
        W["mhalf"] = sb("mhalf", [P, TPG], F32)
        W["eps"] = sb("eps", [P, TPG], F32)
        W["wo_eff"] = sb("wo_eff", [P, KV, DM], F32)
        for n, k, m in (("w1", 1, HID), ("w2", 1, HID), ("h1", 4, HID), ("h2", 4, HID), ("w3", 4, DM)):
            W[n + "h"] = sb(n + "_hi", [P, k, m], F32R)
            W[n + "l"] = sb(n + "_lo", [P, k, m], F32R)
        W["s1"], W["s2"], W["sh1"], W["sh2"] = (sb("scale_" + n, [P, 4], F32) for n in ("w1", "w2", "h1", "h2"))
        W["s3"] = sb("scale_w3", [P, 1], F32)
        W["y"] = sb("y_lat", [P, BATCH * KT, HEADS * LAT], F32)
        prepare(nc, W, x, wqT, wkd, wvd, wkuT, wvuT, wo, w1T, w2T, h1T, h2T, w3T, s1, s2, sh1, sh2, s3,
                q_dram, k_dram, v_dram)
        attend(nc, W, q_dram, k_dram, v_dram)
        finish(nc, W, x, out)


def prepare(nc, W, x, wqT, wkd, wvd, wkuT, wvuT, wo, w1T, w2T, h1T, h2T, w3T, s1, s2, sh1, sh2, s3,
            q_dram, k_dram, v_dram):
    with ExitStack() as ctx:
        sb = lambda name, shape, dt: ctx.enter_context(nc.sbuf_tensor(name, shape, dt))
        sem = lambda name: ctx.enter_context(nc.semaphore(name))
        psum = lambda name, shape: ctx.enter_context(nc.psum_tensor(name, shape, F32))
        wq_sb = sb("wq_sb", [P, HEADS, DM], F32)
        wo_sb = sb("wo_sb", [P, HEADS, DM], F32)
        wku = sb("wku", [P, LAT], F32)
        wvu_pad = sb("wvu_pad", [P, REP, REP, LAT], F32)
        wkd_sb = sb("wkd_sb", [P, KV * LAT], F32)
        wvd_sb = sb("wvd_sb", [P, KV * LAT], F32)
        q_w = sb("q_w", [P, KV, P], F32)
        raw = {n: sb(n + "_raw", [P, k, m], F32)
               for n, k, m in (("w1", 1, HID), ("w2", 1, HID), ("h1", 4, HID), ("h2", 4, HID), ("w3", 4, DM))}
        xs = [sb(f"xs{u}", [P, TPG, DM], F32) for u in range(2)]
        bst = [sb(f"bst{u}", [P, TPG, 6], F32) for u in range(2)]
        mv = [sb(f"mv{u}", [P, TPG, 2], F32) for u in range(2)]
        ve = [sb(f"ve{u}", [P, TPG], F32) for u in range(2)]
        rstd = [sb(f"rstd{u}", [P, TPG], F32) for u in range(2)]
        xn = [sb(f"xn{u}", [P, TPG, DM], F32) for u in range(2)]
        xnT = [sb(f"xnT{u}", [P, GT], F32) for u in range(2)]
        qh = [sb(f"qh{u}", [P, KV, GT], F32R) for u in range(2)]
        ql = [sb(f"ql{u}", [P, KV, GT], F32R) for u in range(2)]
        kh = [sb(f"kh{u}", [KV * LAT, GT], F32R) for u in range(2)]
        kl = [sb(f"kl{u}", [KV * LAT, GT], F32R) for u in range(2)]
        vp = [sb(f"vp{u}", [P, KV, TPG, VC], BF16) for u in range(2)]
        vr = [sb(f"vr{u}", [P, KV, TPG, LAT], F32) for u in range(2)]
        held = sb("held", [P, 1], F32)
        psT = psum("psT", [P, GT])
        psK = psum("psK", [P, GT])
        psQ = [psum(f"psQ{c}", [P, GT]) for c in range(KV)]
        psV = psum("psV", [P, TPG, KV * LAT])
        psA = psum("psA", [P, KV, P])
        psW = psum("psW", [P, KV, P])

        w_loaded = sem("w_loaded")
        ffn_loaded = sem("ffn_loaded")
        consts = sem("consts")
        x_loaded = [sem(f"x_loaded{u}") for u in range(2)]
        mv_ready = sem("mv_ready")
        rstd_ready = sem("rstd_ready")
        xn_ready = sem("xn_ready")
        t_ready = sem("t_ready")
        xnT_ready = sem("xnT_ready")
        proj_ready = sem("proj_ready")
        w_ready = sem("w_ready")
        qw_ready = sem("qw_ready")
        hi_ready = sem("hi_ready")
        lo_ready = sem("lo_ready")
        v_ready = sem("v_ready")
        whi = sem("whi")
        wlo = sem("wlo")
        stored = [sem(f"stored{u}") for u in range(2)]
        d1 = sem("dve_chain")
        p1 = sem("pool_chain")
        v_chain = sem("v_chain")
        names = ("w1", "w2", "h1", "h2", "w3")

        with nc.Block() as block:

            @block.sync
            def _(sp):
                def load_x(j, u):
                    sp.dma_start(xs[u][:, :, :], x[ds(j * GT, GT), :].rearrange("(t p) d -> p t d", p=P))\
                      .then_inc(x_loaded[u], 16)

                load_x(0, 0)
                sp.dma_start(wq_sb[:, :, :], wqT.rearrange("(h d) m -> d h m", d=HD)).then_inc(w_loaded, 16)
                sp.dma_start(wku[:, :], wkuT).then_inc(w_loaded, 16)
                sp.dma_start(wkd_sb[:, :], wkd).then_inc(w_loaded, 16)
                sp.dma_start(wvd_sb[:, :], wvd).then_inc(w_loaded, 16)
                sp.dma_start(wo_sb[:, :, :], wo.rearrange("(h d) m -> d h m", d=HD)).then_inc(w_loaded, 16)
                sp.wait_ge(consts, 1)
                for r in range(REP):
                    sp.dma_start(wvu_pad[:, r, r, :], wvuT).then_inc(w_loaded, 16)
                for n, w in zip(names, (w1T, w2T, h1T, h2T, w3T)):
                    sp.dma_start(raw[n][:, :, :], w.rearrange("(k p) m -> p k m", p=P)).then_inc(ffn_loaded, 16)
                for n, s in (("s1", s1), ("s2", s2), ("sh1", sh1), ("sh2", sh2)):
                    sp.dma_start(W[n][:, :], s).then_inc(ffn_loaded, 16)
                sp.dma_start(W["s3"][:, :], s3).then_inc(ffn_loaded, 16)
                with sp.Fori(0, GROUPS // 2) as i:
                    for u in range(2):
                        sp.wait_ge(xn_ready, 2 * i + 1)
                        load_x((2 * i + u + 1) % GROUPS, 1 - u)
                        tok = ds(sp.snap((2 * i + u) * GT), GT)
                        tiles = ds(sp.snap((2 * i + u) * TPG), TPG)
                        sp.wait_ge(v_ready, 2 * i + u + 1 + 1)
                        for c in range(KV):
                            sp.dma_start(q_dram[1, c * P:(c + 1) * P, tok], ql[u][:, c, :].bitcast(F32)).then_inc(stored[u], 16)
                            sp.dma_start(q_dram[0, c * P:(c + 1) * P, tok], qh[u][:, c, :].bitcast(F32)).then_inc(stored[u], 16)
                        sp.dma_start(k_dram[0, :, tok], kh[u][:, :].bitcast(F32)).then_inc(stored[u], 16)
                        sp.dma_start(k_dram[1, :, tok], kl[u][:, :].bitcast(F32)).then_inc(stored[u], 16)
                        sp.dma_start(v_dram[:, :, tiles, :], vp[u][:, :, :, :])\
                          .then_inc(stored[u], 16)
                for u in range(2):
                    sp.wait_ge(stored[u], STORES * 16 * (GROUPS // 2) + STORES * 16)
                sp.wait_ge(x_loaded[0], 16 * (GROUPS // 2 + 1))
                sp.wait_ge(ffn_loaded, 16 * 10)

            @block.gpsimd
            def _(pool):
                pool.memset(wvu_pad[:, :, :, :], 0.0).then_inc(consts, 1)
                pool.memset(W["mhalf"][:, :], -0.5)
                pool.memset(W["eps"][:, :], EPS)
                pool.memset(W["ident"][:, :], 0.0).then_inc(p1, 1)
                pool.wait_ge(p1, 1)
                pool.affine_select(out=W["ident"][:, :], in_=W["ident"][:, :], compare_op=ALU.not_equal, fill=1.0,
                                   base=0, pattern=[[-1, P]], channel_multiplier=1).then_inc(p1, 1)
                pool.wait_ge(p1, 2)
                pool.tensor_copy(W["identb"][:, :], W["ident"][:, :]).then_inc(consts, 1)

                def rstd_of(j, u):
                    pool.wait_ge(mv_ready, j + 1)
                    pool.tensor_tensor(ve[u][:, :], mv[u][:, :, 1], W["eps"][:, :], ALU.add).then_inc(p1, 1)
                    pool.wait_ge(p1, 2 + j + 1)
                    pool.tensor_tensor(rstd[u][:, :], ve[u][:, :], W["mhalf"][:, :], ALU.pow).then_inc(rstd_ready, 1)

                rstd_of(0, 0)
                with pool.Fori(0, GROUPS // 2) as i:
                    for u in range(2):
                        rstd_of(2 * i + u + 1, 1 - u)
                pool.wait_ge(ffn_loaded, 16 * 10)
                for n, name in enumerate(names):
                    pool.wait_ge(whi, n + 1)
                    pool.tensor_tensor(W[name + "l"][:, :, :], raw[name][:, :, :],
                                       W[name + "h"][:, :, :].bitcast(F32), ALU.subtract).then_inc(wlo, 1)
                pool.wait_ge(wlo, len(names))

            @block.scalar
            def _(act):
                act.wait_ge(qw_ready, 1)
                act.activation(q_w[:, :, :], psA[:, :, :], ACT.Copy).then_inc(w_ready, 1)
                act.wait_ge(qw_ready, 2)
                act.activation(W["wo_eff"][:, :, :], psW[:, :, :], ACT.Copy).then_inc(w_ready, 1)
                with act.Fori(0, GROUPS // 2) as i:
                    for u in range(2):
                        j = 2 * i + u
                        act.wait_ge(t_ready, j + 1)
                        act.activation(xnT[u][:, :], psT[:, :], ACT.Copy).then_inc(xnT_ready, 1)
                        act.wait_ge(stored[u], STORES * 16 * (i + 1))
                        act.wait_ge(proj_ready, 4 * j + 1)
                        act.activation(kh[u][:, :], psK[0:KV * LAT, :], ACT.Copy).then_inc(hi_ready, 1)
                        for c in range(KV):
                            act.wait_ge(proj_ready, 4 * j + 2 + c)
                            act.activation(qh[u][:, c, :], psQ[c][:, :], ACT.Copy).then_inc(hi_ready, 1)
                act.wait_ge(ffn_loaded, 16 * 10)
                for name in names:
                    act.activation(W[name + "h"][:, :, :], raw[name][:, :, :], ACT.Copy).then_inc(whi, 1)

            @block.vector
            def _(dve):
                for u in range(2):
                    dve.memset(vp[u][:, :, :, :], 0.0).then_inc(d1, 1)
                dve.wait_ge(d1, 2)
                for u in range(2):
                    dve.memset(vp[u][:, :, :, LAT:LAT + 1], 1.0).then_inc(d1, 1)
                dve.wait_ge(d1, 4)
                for u in range(2):
                    dve.sem_inc(stored[u], STORES * 16)
                dve.sem_inc(v_ready, 1)

                def norm(j, i, u):
                    dve.wait_ge(x_loaded[u], 16 * (i + 1))
                    for t in range(TPG):
                        last = dve.bn_stats(bst[u][:, t, :], xs[u][:, t, :])
                    last.then_inc(d1, 1)
                    dve.wait_ge(d1, 4 + j + 1)
                    dve.memset(held[:, :], 0.0)
                    for t in range(TPG):
                        last = dve.bn_aggr(mv[u][:, t, :], bst[u][:, t, :])
                    last.then_inc(mv_ready, 1)
                    dve.wait_ge(mv_ready, j + 1)
                    dve.wait_ge(rstd_ready, j + 1)
                    for t in range(TPG):
                        last = dve.tensor_scalar(xn[u][:, t, :], xs[u][:, t, :], mv[u][:, t, 0:1],
                                                 rstd[u][:, t:t + 1], ALU.subtract, ALU.mult)
                    last.then_inc(xn_ready, 1)

                norm(0, 0, 0)
                with dve.Fori(0, GROUPS // 2) as i:
                    for u in range(2):
                        j = 2 * i + u
                        norm(j + 1, i + u, 1 - u)
                        dve.wait_ge(hi_ready, 3 * j + 1)
                        dve.tensor_tensor(kl[u][:, :], psK[0:KV * LAT, :], kh[u][:, :].bitcast(F32), ALU.subtract)\
                           .then_inc(lo_ready, 1)
                        for c in range(KV):
                            dve.wait_ge(hi_ready, 3 * j + 2 + c)
                            dve.tensor_tensor(ql[u][:, c, :], psQ[c][:, :], qh[u][:, c, :].bitcast(F32),
                                              ALU.subtract).then_inc(lo_ready, 1)
                        dve.wait_ge(proj_ready, 4 * j + 4)
                        v = psV[:, :, :].rearrange("p t (c l) -> p c t l", c=KV)
                        part = [vp[u][:, :, :, VW * n:VW * n + LAT] for n in range(VPARTS)]
                        link = Chain(dve, v_chain, 4 * j)
                        link(dve.tensor_copy(part[0], v))
                        link(dve.tensor_tensor(vr[u][:, :, :, :], v, part[0], ALU.subtract))
                        link(dve.tensor_copy(part[1], vr[u][:, :, :, :]))
                        link(dve.tensor_tensor(vr[u][:, :, :, :], vr[u][:, :, :, :], part[1], ALU.subtract))
                        dve.tensor_copy(part[2], vr[u][:, :, :, :]).then_inc(v_ready, 1)

            @block.tensor
            def _(pe):
                pe.wait_ge(w_loaded, 16 * 9)
                for h in range(HEADS):
                    c, r = divmod(h, REP)
                    last = pe.matmul(psA[:, c, r * LAT:(r + 1) * LAT], wq_sb[:, h, :], wku[:, :],
                                     start=True, stop=True)
                last.then_inc(qw_ready, 1)
                for c in range(KV):
                    for r in range(REP):
                        last = pe.matmul(psW[:, c, :], wvu_pad[:, r, :, :].rearrange("p a l -> p (a l)"),
                                         wo_sb[:, c * REP + r, :], start=(r == 0), stop=(r == REP - 1))
                last.then_inc(qw_ready, 1)
                pe.wait_ge(consts, 2)
                pe.wait_ge(w_ready, 1)
                with pe.Fori(0, GROUPS // 2) as i:
                    for u in range(2):
                        j = 2 * i + u
                        pe.wait_ge(xn_ready, j + 1)
                        for t in range(TPG):
                            last = pe.transpose(psT[:, t * P:(t + 1) * P], xn[u][:, t, :], W["ident"][:, :])
                        last.then_inc(t_ready, 1)
                        pe.wait_ge(xnT_ready, j + 1)
                        pe.wait_ge(v_ready, j + 1)
                        pe.matmul(psK[0:KV * LAT, :], wkd_sb[:, :], xnT[u][:, :], start=True, stop=True)\
                          .then_inc(proj_ready, 1)
                        for c in range(KV):
                            pe.matmul(psQ[c][:, :], q_w[:, c, :], xnT[u][:, :], start=True, stop=True)\
                              .then_inc(proj_ready, 1)
                        for t in range(TPG):
                            last = pe.matmul(psV[:, t, :], xnT[u][:, t * P:(t + 1) * P], wvd_sb[:, :],
                                             start=True, stop=True)
                        last.then_inc(proj_ready, 1)


LAG = 3
NP_BUF = 4
JOBS = BATCH * QG
LEAD = 20


class Pair:

    def __init__(self, job, first):
        self.job, self.e, self.g = job, job // QG, job % QG
        self.tiles, at = [], 0
        for kt in (first, first + 1):
            q0 = max(0, kt - TPG * self.g) * P
            self.tiles.append((kt, q0, at, kt >= TPG * self.g))
            at += GT - q0
        self.width = at
        self.first = first == 0
        self.last = first + 2 == TPG * (self.g + 1)


PAIRS = [Pair(job, first) for job in range(JOBS) for first in range(0, TPG * (job % QG + 1), 2)]
STEPS = len(PAIRS)
CHUNKS = [(job, t, c, GT if c < job % QG else (t + 1) * P)
          for job in range(JOBS) for t in range(TPG) for c in range(job % QG + 1)]
NCH = len(CHUNKS)


def plan():
    share = [[] for _ in range(STEPS + LAG + 1)]
    at = LEAD
    for k in range(STEPS):
        while at < min(LEAD + 2 * (k + 1), NCH):
            share[k].append(at)
            at += 1
    rest = [k for k in range(len(share)) if not share[k]]
    for n in range(LEAD):
        share[rest[n * len(rest) // LEAD]].append(NCH + n)
    return share


SHARE = plan()


def on_vector(k):
    return k % 4 == 3


def attend(nc, W, q_dram, k_dram, v_dram):
    with ExitStack() as ctx:
        sb = lambda name, shape, dt: ctx.enter_context(nc.sbuf_tensor(name, shape, dt))
        sem = lambda name: ctx.enter_context(nc.semaphore(name))
        psum = lambda name, shape: ctx.enter_context(nc.psum_tensor(name, shape, F32))
        qs = [sb(f"qs{e}", [P, SEQ], F32R) for e in range(BATCH)]
        ks = [sb(f"ks{e}", [P, SEQ], F32R) for e in range(BATCH)]
        vs = [sb(f"vs{e}", [P, KT, VC], BF16) for e in range(BATCH)]
        prob = [sb(f"prob{n}", [P, 2 * GT], F32) for n in range(NP_BUF)]
        rest = [sb(f"rest{n}", [P, 2 * GT], F16) for n in range(NP_BUF)]
        acc_sb = [sb(f"acc_sb{n}", [VC, GT], F32) for n in range(2)]
        mask_q = sb("mask_q", [P, P], BF16)
        mask_k = sb("mask_k", [P, P], BF16)
        fold = sb("fold", [VC, VW], F32)
        shift = sb("shift", [P, 1], F32)
        mpart = [sb(f"mpart{n}", [P, TPG, QG], F32) for n in range(2)]
        nmax = sb("nmax", [P, TPG], F32)
        nmax_hi = sb("nmax_hi", [P, TPG], F32R)
        mcols = sb("mcols", [P, TPG, P], F32)
        rden = sb("rden", [P, TPG], F32)
        s_max = [psum(f"s_max{n}", [P, GT]) for n in range(2)]
        s_t = [psum(f"s_t{n}", [P, 2 * GT]) for n in range(2)]
        acc = psum("acc", [P, GT])
        misc = psum("misc", [P, TPG, P])

        qk_loaded = [sem(f"qk_loaded{e}") for e in range(BATCH)]
        v_loaded = [sem(f"v_loaded{e}") for e in range(BATCH)]
        consts = sem("a_consts")
        pool_chain = sem("a_pool_chain")
        smax_ready = sem("smax_ready")
        max_done = sem("max_done")
        fin_chain = sem("fin_chain")
        nmax_ready = sem("nmax_ready")
        mt_ready = sem("mt_ready")
        mrow_ready = sem("mrow_ready")
        st_ready = sem("st_ready")
        exp_done = sem("exp_done")
        rest_pool = sem("rest_pool")
        rest_dve = sem("rest_dve")
        pv_done = sem("pv_done")
        acc_copied = sem("acc_copied")
        fold_ready = sem("fold_ready")
        y_chain = sem("y_chain")
        y_done = sem("y_done")
        DVE_PAIRS = [k for k in range(STEPS) if on_vector(k)]
        POOL_PAIRS = [k for k in range(STEPS) if not on_vector(k)]
        FREE_MAX, FREE_ST, FREE_P = 2, 2, NP_BUF

        def chunk_of(n, h):
            ahead = n >= NCH
            return CHUNKS[n % NCH], h + (1 if ahead else 0), h * NCH + n

        def ends_job(n):
            return n % NCH == NCH - 1 or CHUNKS[(n + 1) % NCH][0] != CHUNKS[n % NCH][0]

        MT = [[] for _ in range(len(SHARE) + 1)]
        for k, share in enumerate(SHARE):
            for n in share:
                if ends_job(n):
                    MT[min(k + 1, len(SHARE) - 1)].append((n // NCH, CHUNKS[n % NCH][0]))
        PRE = [n for n in range(LEAD)]
        PRE_MT = [(0, CHUNKS[n][0]) for n in PRE if ends_job(n)]

        def fold_job(k):
            n = k - LAG - 1
            return PAIRS[n].job if 0 <= n < STEPS and PAIRS[n].last else None

        def jobs_of(mt, h, last):
            for ahead, job in mt:
                if not (ahead and last):
                    yield job, (h + ahead) * JOBS + job

        def share_of(k, last):
            return [n for n in SHARE[k] if not (last and n >= NCH)]

        def heads(eng, body):
            with eng.Fori(0, HEADS - 1) as h:
                body(h, False)
            body(HEADS - 1, True)

        with nc.Block() as block:

            @block.sync
            def _(sp):
                def load(h, e):
                    tok = slice(e * SEQ, (e + 1) * SEQ)
                    row = h * LAT
                    krow = (h // REP) * LAT
                    for n, part in enumerate((0, 0, 1)):
                        sp.dma_start(qs[e][n * LAT:(n + 1) * LAT, :].bitcast(F32), q_dram[part, ds(row, LAT), tok])\
                          .then_inc(qk_loaded[e], 16)
                    for n, part in enumerate((0, 1, 0)):
                        sp.dma_start(ks[e][n * LAT:(n + 1) * LAT, :].bitcast(F32), k_dram[part, ds(krow, LAT), tok])\
                          .then_inc(qk_loaded[e], 16)
                    sp.dma_start(vs[e][:, :, :], v_dram[:, ds(h // REP, 1), e * KT:(e + 1) * KT, :]
                                 .rearrange("p o t c -> p (o t) c")).then_inc(v_loaded[e], 16)

                for e in range(BATCH):
                    load(0, e)
                with sp.Fori(0, HEADS - 1) as h:
                    for e in range(BATCH):
                        sp.wait_ge(pv_done, FREE_P + h * STEPS + STEPS // BATCH * (e + 1))
                        load(h + 1, e)

            @block.gpsimd
            def _(pool):
                link = Chain(pool, pool_chain)
                link(pool.memset(mask_q[:, :], 0.0))
                link(pool.affine_select(out=mask_q[:, :], in_=mask_q[:, :], compare_op=ALU.is_ge, fill=NEG,
                                        base=0, pattern=[[-1, P]], channel_multiplier=1))
                link(pool.memset(mask_k[:, :], 0.0))
                link(pool.affine_select(out=mask_k[:, :], in_=mask_k[:, :], compare_op=ALU.is_ge, fill=NEG,
                                        base=0, pattern=[[1, P]], channel_multiplier=-1))
                link(pool.memset(fold[:, :], 0.0))
                for n in range(VPARTS):
                    link(pool.affine_select(out=fold[:, :], in_=fold[:, :], compare_op=ALU.not_equal, fill=1.0,
                                            base=-n * VW, pattern=[[-1, VW]], channel_multiplier=1))
                pool.sem_inc(consts, 1)

                def body(h, last):
                    for k in range(STEPS):
                        if not on_vector(k):
                            pr, width = k % NP_BUF, PAIRS[k].width
                            pool.wait_ge(exp_done, FREE_ST + h * STEPS + k + 1)
                            pool.tensor_tensor(rest[pr][:, 0:width], prob[pr][:, 0:width],
                                               prob[pr][:, 0:width].bitcast(BF16)[:, 1::2], ALU.subtract)\
                                .then_inc(rest_pool, 1)
                heads(pool, body)

            @block.scalar
            def _(act):
                act.sem_inc(exp_done, FREE_ST)
                act.sem_inc(acc_copied, 1)

                def mrow(job, number):
                    e, g = divmod(job, QG)
                    act.wait_ge(mt_ready, number + 1)
                    act.activation(qs[e][SROWS:P, g * GT:(g + 1) * GT],
                                   misc[SROWS:P, :, :].rearrange("p t q -> p (t q)"), ACT.Copy)\
                       .then_inc(mrow_ready, 1)

                def body(h, last):
                    for k in range(len(SHARE)):
                        if k < STEPS:
                            n = h * STEPS + k
                            act.wait_ge(st_ready, n + 1)
                            act.wait_ge(pv_done, n + 1)
                            act.activation(prob[k % NP_BUF][:, 0:PAIRS[k].width], s_t[k % 2][:, 0:PAIRS[k].width],
                                           ACT.Exp, bias=shift[:, 0:1], scale=SCALE).then_inc(exp_done, 1)
                        for job, number in jobs_of(MT[k], h, last):
                            mrow(job, number)
                        m = k - LAG
                        if 0 <= m < STEPS and PAIRS[m].last:
                            act.wait_ge(pv_done, FREE_P + h * STEPS + m + 1)
                            act.activation(acc_sb[PAIRS[m].job % 2][:, :], acc[0:VC, :], ACT.Copy)\
                               .then_inc(acc_copied, 1)

                act.wait_ge(consts, 2)
                for _, job in PRE_MT:
                    mrow(job, job)
                heads(act, body)

            @block.vector
            def _(dve):
                for e in range(BATCH):
                    dve.memset(ks[e][SROWS:P, :].bitcast(F32), 0.0).then_inc(fin_chain, 1)
                dve.memset(mcols[:, :, :], 0.0)
                dve.memset(shift[:, :], PSHIFT).then_inc(fin_chain, 1)
                dve.wait_ge(fin_chain, 3)
                for e in range(BATCH):
                    dve.memset(ks[e][SROWS:SROWS + 2, :].bitcast(F32), 1.0).then_inc(fin_chain, 1)
                dve.wait_ge(fin_chain, 5)
                dve.sem_inc(consts, 1)
                dve.sem_inc(max_done, FREE_MAX)
                dve.sem_inc(y_done, 1)

                def maximum(n, h):
                    (job, t, c, width), _, number = chunk_of(n, h)
                    dve.wait_ge(smax_ready, number + 1)
                    dve.reduce_max(mpart[job % 2][:, t, c:c + 1], s_max[n % 2][:, 0:width], AX.X)\
                       .then_inc(max_done, 1)
                    if ends_job(n):
                        jn = h * JOBS + job + (JOBS if n >= NCH else 0)
                        dve.wait_ge(max_done, FREE_MAX + number + 1)
                        link = Chain(dve, fin_chain, 5 + 2 * jn)
                        link(dve.tensor_reduce(nmax[:, :], mpart[job % 2][:, :, 0:job % QG + 1], AX.X, ALU.max,
                                               negate=True))
                        link(dve.tensor_copy(nmax_hi[:, :], nmax[:, :]))
                        if not (isinstance(jn, int) and jn == 0):
                            dve.wait_ge(mt_ready, jn)
                        dve.tensor_copy(mcols[:, :, SROWS], nmax[:, :])
                        dve.tensor_tensor(mcols[:, :, SROWS + 1], nmax[:, :], nmax_hi[:, :].bitcast(F32),
                                          ALU.subtract).then_inc(nmax_ready, 1)

                def weigh(job, number, h):
                    e, g = divmod(job, QG)
                    dve.wait_ge(fold_ready, number + 1)
                    dve.reciprocal(rden[:, :], misc[:, :, LAT]).then_inc(y_chain, 1)
                    dve.wait_ge(y_chain, number + 1)
                    dve.tensor_tensor(W["y"][:, e * KT + g * TPG:e * KT + (g + 1) * TPG, ds(h * LAT, LAT)],
                                      misc[:, :, 0:LAT], rden[:, :].unsqueeze(2).to_broadcast([P, TPG, LAT]),
                                      ALU.mult).then_inc(y_done, 1)

                def body(h, last):
                    for k in range(len(SHARE)):
                        for n in share_of(k, last):
                            maximum(n, h)
                        if 0 <= k - 1 < STEPS and on_vector(k - 1):
                            m = k - 1
                            pr, width = m % NP_BUF, PAIRS[m].width
                            dve.wait_ge(exp_done, FREE_ST + h * STEPS + m + 1)
                            dve.tensor_tensor(rest[pr][:, 0:width], prob[pr][:, 0:width],
                                              prob[pr][:, 0:width].bitcast(BF16)[:, 1::2], ALU.subtract)\
                               .then_inc(rest_dve, 1)
                        job = fold_job(k)
                        if job is not None:
                            weigh(job, h * JOBS + job, h)

                for n in PRE:
                    maximum(n, 0)
                heads(dve, body)

            @block.tensor
            def _(pe):
                pe.sem_inc(pv_done, FREE_P)

                def scores_q(n, h):
                    (job, t, c, width), hh, number = chunk_of(n, h)
                    e, g = divmod(job, QG)
                    if n % NCH in (0, NCH // BATCH):
                        pe.wait_ge(qk_loaded[e], 6 * 16 * (hh + 1))
                    pe.wait_ge(max_done, number + 1)
                    bank = s_max[n % 2]
                    diagonal = c == g
                    q = (g * TPG + t) * P
                    last = pe.matmul(bank[:, 0:width], qs[e][0:SROWS, q:q + P],
                                     ks[e][0:SROWS, c * GT:c * GT + width], start=True, stop=not diagonal)
                    if diagonal:
                        last = pe.matmul(bank[:, width - P:width], W["identb"][:, :], mask_q[:, :],
                                         start=False, stop=True)
                    last.then_inc(smax_ready, 1)

                def turn_maxima(job, number):
                    pe.wait_ge(nmax_ready, number + 1)
                    pe.wait_ge(y_done, folds[0] + 1)
                    if not (isinstance(number, int) and number == 0):
                        pe.wait_ge(mrow_ready, number)
                    for t in range(TPG):
                        last = pe.transpose(misc[:, t, :], mcols[:, t, :], W["ident"][:, :])
                    last.then_inc(mt_ready, 1)

                folds = [0]

                def body(h, last):
                    for k in range(len(SHARE)):
                        if k < STEPS:
                            pair = PAIRS[k]
                            if pair.first:
                                pe.wait_ge(mrow_ready, h * JOBS + pair.job + 1)
                            pe.wait_ge(exp_done, h * STEPS + k + 1)
                            for kt, q0, at, diagonal in pair.tiles:
                                width = GT - q0
                                mm = pe.matmul(s_t[k % 2][:, at:at + width], ks[pair.e][:, kt * P:(kt + 1) * P],
                                               qs[pair.e][:, pair.g * GT + q0:(pair.g + 1) * GT],
                                               start=True, stop=not diagonal)
                                if diagonal:
                                    mm = pe.matmul(s_t[k % 2][:, at:at + P], W["identb"][:, :], mask_k[:, :],
                                                   start=False, stop=True)
                            mm.then_inc(st_ready, 1)
                        for n in share_of(k, last):
                            scores_q(n, h)
                        folds[0] = h * JOBS + sum(1 for m in range(k) if fold_job(m) is not None)
                        for job, number in jobs_of(MT[k], h, last):
                            turn_maxima(job, number)
                        m = k - LAG
                        if 0 <= m < STEPS:
                            pair, n = PAIRS[m], h * STEPS + m
                            if m in (0, STEPS // BATCH):
                                pe.wait_ge(v_loaded[pair.e], 16 * (h + 1))
                            if pair.first:
                                pe.wait_ge(acc_copied, h * JOBS + pair.job + 1)
                            if on_vector(m):
                                pe.wait_ge(rest_dve, h * len(DVE_PAIRS) + DVE_PAIRS.index(m) + 1)
                            else:
                                pe.wait_ge(rest_pool, h * len(POOL_PAIRS) + POOL_PAIRS.index(m) + 1)
                            high = prob[m % NP_BUF][:, :].bitcast(BF16)[:, 1::2]
                            for half, (kt, q0, at, _) in enumerate(pair.tiles):
                                v = vs[pair.e][:, kt, :]
                                end = pair.last and half == 1
                                pe.matmul(acc[0:VC, q0:GT], v, high[:, at:at + GT - q0],
                                          start=(pair.first and half == 0), stop=False)
                                mm = pe.matmul(acc[0:VC, q0:GT], v, rest[m % NP_BUF][:, at:at + GT - q0],
                                               start=False, stop=end)
                            mm.then_inc(pv_done, 1)
                        job = fold_job(k)
                        if job is not None:
                            number = h * JOBS + job
                            pe.wait_ge(acc_copied, 1 + number + 1)
                            pe.wait_ge(y_done, number + 1)
                            pe.wait_ge(mrow_ready, turned(h, k, last))
                            for t in range(TPG):
                                mm = pe.matmul(misc[:, t, 0:VW], acc_sb[job % 2][:, t * P:(t + 1) * P], fold[:, :],
                                               start=True, stop=True)
                            mm.then_inc(fold_ready, 1)

                def turned(h, k, last):
                    return len(PRE_MT) + h * JOBS + sum(len(list(jobs_of(MT[m], 0, last))) for m in range(k + 1))

                pe.wait_ge(consts, 2)
                folds[0] = 0
                for n in range(LEAD + 2):
                    if n < LEAD:
                        scores_q(n, 0)
                    if n >= 2 and ends_job(n - 2):
                        turn_maxima(CHUNKS[n - 2][0], CHUNKS[n - 2][0])
                heads(pe, body)


def finish(nc, W, x, out):
    with ExitStack() as ctx:
        sb = lambda name, shape, dt: ctx.enter_context(nc.sbuf_tensor(name, shape, dt))
        sem = lambda name: ctx.enter_context(nc.semaphore("f_" + name))
        psum = lambda name, shape: ctx.enter_context(nc.psum_tensor(name, shape, F32))
        MT = HID // P
        two = range(2)
        xs = [sb(f"f_xs{u}", [P, TPG, DM], F32) for u in two]
        ys = [sb(f"f_ys{u}", [P, TPG, HEADS * LAT], F32) for u in two]
        yT = sb("f_yT", [P, KV, GT], F32)
        stats = {n: sb(f"f_stats_{n}", [P, TPG, 6], F32) for n in "abo"}
        mv = {n: sb(f"f_mv_{n}", [P, TPG, 2], F32) for n in "abo"}
        ve = {n: sb(f"f_ve_{n}", [P, TPG], F32) for n in "abo"}
        rstd = {n: sb(f"f_rstd_{n}", [P, TPG], F32) for n in "abo"}
        nrm = sb("f_nrm", [P, TPG, DM], F32)
        x1 = [sb(f"f_x1{u}", [P, TPG, DM], F32) for u in two]
        xn = sb("f_xn", [P, TPG, DM], F32)
        xh = [sb(f"f_xh{u}", [P, GT], F32R) for u in two]
        xl = [sb(f"f_xl{u}", [P, GT], F32R) for u in two]
        sg = [sb(f"f_sg{n}", [P, GT], F32) for n in two]
        full = [sb(f"f_full{n}", [P, GT], F32) for n in two]
        hi = [sb(f"f_hi{n}", [P, MT, GT], F32R) for n in two]
        lo = [sb(f"f_lo{n}", [P, MT, GT], F32R) for n in two]
        oT = sb("f_oT", [P, GT], F32)
        held = sb("f_held", [P, 1], F32)
        on = [sb(f"f_on{u}", [P, TPG, DM], F32) for u in two]
        res = [sb(f"f_res{u}", [P, TPG, DM], F32) for u in two]
        ring = [psum(f"f_ring{n}", [P, GT]) for n in range(4)]
        psY = [psum(f"f_psY{c}", [P, TPG, P]) for c in range(KV)]
        psX = psum("f_psX", [P, TPG, DM])
        psN = psum("f_psN", [P, GT])

        loaded = [sem(f"loaded{u}") for u in two]
        y_turned, yT_ready, ao_ready = sem("y_turned"), sem("yT_ready"), sem("ao_ready")
        st = {n: sem(f"stats_{n}") for n in "abo"}
        mv_ready = {n: sem(f"mv_ready_{n}") for n in "abo"}
        rs = {n: sem(f"rstd_{n}") for n in "abo"}
        pc = {n: sem(f"pool_{n}") for n in "abo"}
        nrm_ready, x1_ready, xn_ready = sem("nrm_ready"), sem("x1_ready"), sem("xn_ready")
        n_turned, xh_ready, xl_ready = sem("n_turned"), sem("xh_ready"), sem("xl_ready")
        in_ready, silu_done, prod_done = sem("in_ready"), sem("silu_done"), sem("prod_done")
        hid_ready, gelu_done, hi_ready, lo_ready = sem("hid_ready"), sem("gelu_done"), sem("hi_ready"), sem("lo_ready")
        o_ready, oT_ready, o_turned, on_ready = sem("o_ready"), sem("oT_ready"), sem("o_turned"), sem("on_ready")
        res_ready = sem("res_ready")
        stored = [sem(f"stored{u}") for u in two]
        LAYERS = 3
        PARTS = LAYERS * MT

        def groups(eng, body):
            with eng.Fori(0, GROUPS // 2) as i:
                for u in two:
                    body(i, 2 * i + u, u)

        with nc.Block() as block:

            @block.sync
            def _(sp):
                def load(j, u):
                    sp.dma_start(xs[u][:, :, :], x[ds(j * GT, GT), :].rearrange("(t p) d -> p t d", p=P))\
                      .then_inc(loaded[u], 16)
                    sp.dma_start(ys[u][:, :, :], W["y"][:, ds(j * TPG, TPG), :]).then_inc(loaded[u], 16)

                load(0, 0)

                def body(i, j, u):
                    sp.wait_ge(x1_ready, j + 1)
                    load((j + 1) % GROUPS, 1 - u)
                    sp.wait_ge(res_ready, j + 1)
                    sp.dma_start(out[ds(j * GT, GT), :].rearrange("(t p) d -> p t d", p=P), res[u][:, :, :])\
                      .then_inc(stored[u], 16)
                groups(sp, body)
                for u in two:
                    sp.wait_ge(stored[u], 16 * (GROUPS // 2 + 1))

            @block.gpsimd
            def _(pool):
                for u in two:
                    pool.sem_inc(stored[u], 16)

                def rstd_of(n, j):
                    pool.wait_ge(mv_ready[n], j + 1)
                    pool.tensor_tensor(ve[n][:, :], mv[n][:, :, 1], W["eps"][:, :], ALU.add).then_inc(pc[n], 1)
                    pool.wait_ge(pc[n], j + 1)
                    pool.tensor_tensor(rstd[n][:, :], ve[n][:, :], W["mhalf"][:, :], ALU.pow).then_inc(rs[n], 1)

                def front(j, i, u):
                    rstd_of("a", j)
                    pool.wait_ge(nrm_ready, j + 1)
                    pool.tensor_tensor(x1[u][:, :, :], xs[u][:, :, :], nrm[:, :, :], ALU.add).then_inc(x1_ready, 1)
                    rstd_of("b", j)

                pool.wait_ge(loaded[0], 32)
                front(0, 0, 0)

                def body(i, j, u):
                    pool.wait_ge(loaded[1 - u], 32 * (i + u + 1))
                    front(j + 1, i + u, 1 - u)
                    rstd_of("o", j)
                    pool.wait_ge(on_ready, 1 + j + 1)
                    pool.wait_ge(stored[u], 16 * (i + 1))
                    pool.tensor_tensor(res[u][:, :, :], x1[u][:, :, :], on[u][:, :, :], ALU.add)\
                        .then_inc(res_ready, 1)
                groups(pool, body)

            @block.scalar
            def _(act):
                act.sem_inc(oT_ready, 1)

                def y_out(j):
                    for c in range(KV):
                        act.wait_ge(y_turned, KV * j + c + 1)
                        act.activation(yT[:, c, :], psY[c][:, :, :].rearrange("p t q -> p (t q)"), ACT.Copy)\
                           .then_inc(yT_ready, 1)

                def n_out(j, u):
                    act.wait_ge(n_turned, j + 1)
                    act.activation(xh[u][:, :], psN[:, :], ACT.Copy).then_inc(xh_ready, 1)

                y_out(0)
                n_out(0, 0)

                def body(i, j, u):
                    def high(m):
                        act.wait_ge(prod_done, MT * j + m + 1)
                        act.activation(hi[0][:, m, :], full[m % 2][:, :], ACT.Copy).then_inc(hi_ready, 1)

                    for m in range(MT):
                        act.wait_ge(in_ready, 2 * (MT * j + m) + 1)
                        if m >= 2:
                            act.wait_ge(prod_done, MT * j + m - 1)
                        act.activation(sg[m % 2][:, :], ring[2 * m % 4][:, :], ACT.Silu, scale=W["s1"][:, m:m + 1])\
                           .then_inc(silu_done, 1)
                        if m >= 1:
                            high(m - 1)
                    high(MT - 1)
                    y_out(j + 1)
                    for layer, scale in ((1, "sh1"), (2, "sh2")):
                        for m in range(MT):
                            act.wait_ge(hid_ready, 2 * MT * j + (layer - 1) * MT + m + 1)
                            s = W[scale][:, m:m + 1]
                            act.activation(hi[layer % 2][:, m, :], ring[m][:, :], ACT.Gelu, scale=s)\
                               .then_inc(hi_ready, 1)
                            act.wait_ge(lo_ready, PARTS * j + layer * MT + m - 1)
                            act.activation(full[m % 2][:, :], ring[m][:, :], ACT.Gelu, scale=s)\
                               .then_inc(gelu_done, 1)
                    act.wait_ge(o_ready, j + 1)
                    act.activation(oT[:, :], ring[0][:, :], ACT.Copy, scale=W["s3"][:, 0:1]).then_inc(oT_ready, 1)
                    n_out(j + 1, 1 - u)
                groups(act, body)

            @block.vector
            def _(dve):
                dve.sem_inc(on_ready, 1)

                def moments(n, j, src):
                    for t in range(TPG):
                        last = dve.bn_stats(stats[n][:, t, :], src[:, t, :])
                    last.then_inc(st[n], 1)
                    dve.wait_ge(st[n], j + 1)
                    dve.memset(held[:, :], 0.0)
                    for t in range(TPG):
                        last = dve.bn_aggr(mv[n][:, t, :], stats[n][:, t, :])
                    last.then_inc(mv_ready[n], 1)

                def normalise(n, j, dst, src, done):
                    dve.wait_ge(mv_ready[n], j + 1)
                    dve.wait_ge(rs[n], j + 1)
                    for t in range(TPG):
                        last = dve.tensor_scalar(dst[:, t, :], src[:, t, :], mv[n][:, t, 0:1],
                                                 rstd[n][:, t:t + 1], ALU.subtract, ALU.mult)
                    last.then_inc(done, 1)

                def front(j, u):
                    def first():
                        dve.wait_ge(ao_ready, j + 1)
                        moments("a", j, psX)

                    def second():
                        normalise("a", j, nrm, psX, nrm_ready)

                    def third():
                        dve.wait_ge(x1_ready, j + 1)
                        moments("b", j, x1[u])

                    def fourth():
                        normalise("b", j, xn, x1[u], xn_ready)
                    return first, second, third, fourth

                def n_low(j, u):
                    dve.wait_ge(xh_ready, j + 1)
                    dve.tensor_tensor(xl[u][:, :], psN[:, :], xh[u][:, :].bitcast(F32), ALU.subtract)\
                       .then_inc(xl_ready, 1)

                for step in front(0, 0):
                    step()
                n_low(0, 0)

                def body(i, j, u):
                    def low(layer, m):
                        dve.wait_ge(hi_ready, PARTS * j + layer * MT + m + 1)
                        if layer:
                            dve.wait_ge(gelu_done, 2 * MT * j + (layer - 1) * MT + m + 1)
                        dve.tensor_tensor(lo[layer % 2][:, m, :], full[m % 2][:, :],
                                          hi[layer % 2][:, m, :].bitcast(F32), ALU.subtract).then_inc(lo_ready, 1)

                    for m in range(MT):
                        dve.wait_ge(in_ready, 2 * (MT * j + m) + 2)
                        if m >= 2:
                            dve.wait_ge(lo_ready, PARTS * j + m - 1)
                        dve.wait_ge(silu_done, MT * j + m + 1)
                        dve.scalar_tensor_tensor(out=full[m % 2][:, :], in0=ring[2 * m % 4 + 1][:, :],
                                                 scalar=W["s2"][:, m:m + 1], in1=sg[m % 2][:, :],
                                                 op0=ALU.mult, op1=ALU.mult).then_inc(prod_done, 1)
                        if m >= 1:
                            low(0, m - 1)
                    low(0, MT - 1)
                    for m in range(MT):
                        low(1, m)
                    for m, step in zip(range(MT), front(j + 1, 1 - u)):
                        step()
                        low(2, m)
                    n_low(j + 1, 1 - u)
                    dve.wait_ge(o_turned, j + 1)
                    moments("o", j, psY[0])
                    normalise("o", j, on[u], psY[0], on_ready)
                groups(dve, body)

            @block.tensor
            def _(pe):
                def y_turn(u):
                    for c in range(KV):
                        for t in range(TPG):
                            last = pe.transpose(psY[c][:, t, :], ys[u][:, t, c * P:(c + 1) * P], W["ident"][:, :])
                        last.then_inc(y_turned, 1)

                def project(j):
                    pe.wait_ge(yT_ready, KV * (j + 1))
                    for t in range(TPG):
                        for c in range(KV):
                            last = pe.matmul(psX[:, t, :], yT[:, c, t * P:(t + 1) * P], W["wo_eff"][:, c, :],
                                             start=(c == 0), stop=(c == KV - 1))
                    last.then_inc(ao_ready, 1)

                def n_turn(j):
                    pe.wait_ge(xn_ready, j + 1)
                    for t in range(TPG):
                        last = pe.transpose(psN[:, t * P:(t + 1) * P], xn[:, t, :], W["ident"][:, :])
                    last.then_inc(n_turned, 1)

                def product(bank, w, k, m, high, low, first, last):
                    wh, wl = (W[w + p][:, k, m * P:(m + 1) * P] for p in "hl")
                    pe.matmul(bank, wh, high, start=first, stop=False)
                    pe.matmul(bank, wl, high, start=False, stop=False)
                    return pe.matmul(bank, wh, low, start=False, stop=last)

                pe.wait_ge(loaded[0], 32)
                y_turn(0)
                project(0)
                n_turn(0)

                def body(i, j, u):
                    pe.wait_ge(xh_ready, j + 1)
                    pe.wait_ge(xl_ready, j + 1)
                    pe.wait_ge(oT_ready, j + 1)
                    for m in range(MT):
                        if m >= 2:
                            pe.wait_ge(prod_done, MT * j + m - 1)
                        for n, w in enumerate(("w1", "w2")):
                            product(ring[2 * m % 4 + n][:, :], w, 0, m, xh[u][:, :], xl[u][:, :], True, True)\
                                .then_inc(in_ready, 1)
                    pe.wait_ge(loaded[1 - u], 32 * (i + u + 1))
                    pe.wait_ge(on_ready, j + 1)
                    y_turn(1 - u)
                    for layer, w in ((1, "h1"), (2, "h2")):
                        for m in range(MT):
                            if layer == 1 and m in (0, 2):
                                pe.wait_ge(prod_done, MT * j + 3 + m // 2)
                            for k in range(MT):
                                if m == 0:
                                    pe.wait_ge(hi_ready, PARTS * j + (layer - 1) * MT + k + 1)
                                    pe.wait_ge(lo_ready, PARTS * j + (layer - 1) * MT + k + 1)
                                last = product(ring[m][:, :], w, k, m, hi[(layer - 1) % 2][:, k, :],
                                               lo[(layer - 1) % 2][:, k, :], k == 0, k == MT - 1)
                            last.then_inc(hid_ready, 1)
                        if layer == 1:
                            project(j + 1)
                    for k in range(MT):
                        pe.wait_ge(hi_ready, PARTS * j + 2 * MT + k + 1)
                        pe.wait_ge(lo_ready, PARTS * j + 2 * MT + k + 1)
                        last = product(ring[0][:, :], "w3", k, 0, hi[0][:, k, :], lo[0][:, k, :],
                                       k == 0, k == MT - 1)
                    last.then_inc(o_ready, 1)
                    n_turn(j + 1)
                    pe.wait_ge(oT_ready, 1 + j + 1)
                    for t in range(TPG):
                        last = pe.transpose(psY[0][:, t, :], oT[:, t * P:(t + 1) * P], W["ident"][:, :])
                    last.then_inc(o_turned, 1)
                groups(pe, body)


def kernel(L0_attn_x, L0_attn_wq, L0_attn_wk_down, L0_attn_wv_down, L0_attn_wk_up, L0_attn_wv_up, L0_attn_wo,
           L0_ffn_w1_w, L0_ffn_w1_s, L0_ffn_w2_w, L0_ffn_w2_s, L0_ffn_h1_w, L0_ffn_h1_s, L0_ffn_h2_w, L0_ffn_h2_s,
           L0_ffn_w3_w, L0_ffn_w3_s):
    import concourse.bacc as bacc
    from concourse.bass_utils import run_bass_kernel_spmd

    f = lambda a: np.ascontiguousarray(np.asarray(a))
    column = lambda s: f(np.asarray(s).reshape(-1, P).T)
    ins = {
        "x": f(L0_attn_x).reshape(TOK, DM), "wqT": f(np.asarray(L0_attn_wq).T), "wkd": f(L0_attn_wk_down),
        "wvd": f(L0_attn_wv_down), "wkuT": f(np.asarray(L0_attn_wk_up).T), "wvuT": f(np.asarray(L0_attn_wv_up).T),
        "wo": f(L0_attn_wo), "w1T": f(np.asarray(L0_ffn_w1_w).T), "w2T": f(np.asarray(L0_ffn_w2_w).T),
        "h1T": f(np.asarray(L0_ffn_h1_w).T), "h2T": f(np.asarray(L0_ffn_h2_w).T),
        "w3T": f(np.asarray(L0_ffn_w3_w).T), "s1": column(L0_ffn_w1_s), "s2": column(L0_ffn_w2_s),
        "sh1": column(L0_ffn_h1_s), "sh2": column(L0_ffn_h2_s), "s3": column(L0_ffn_w3_s),
    }
    nc = bacc.Bacc("TRN2", target_bir_lowering=False, num_devices=1)
    aps = {n: nc.dram_tensor("in_" + n, a.shape, F32, kind="ExternalInput").ap() for n, a in ins.items()}
    out = nc.dram_tensor("out_0", (TOK, DM), F32, kind="ExternalOutput").ap()
    layer(nc, *[aps[n] for n in ins], out)
    r = run_bass_kernel_spmd(nc, [{"in_" + n: a for n, a in ins.items()}], core_ids=[0])
    return r.results[0]["out_0"].reshape(BATCH, SEQ, DM)
```

```python
import numpy as np
import concourse.bass as bass
from concourse import mybir
from contextlib import ExitStack

F32 = mybir.dt.float32
F32R = mybir.dt.float32r
BF16 = mybir.dt.bfloat16
F16 = mybir.dt.float16
ALU = mybir.AluOpType
ACT = mybir.ActivationFunctionType
AX = mybir.AxisListType
ds = bass.ds

P = 128
BATCH, SEQ, DM = 2, 2048, 128
TOK = BATCH * SEQ
HEADS, KV, HD, LAT = 8, 2, 128, 32
REP = HEADS // KV
HID = 512
FFN_W, FFN_COLS = {}, 0
for _name, _in, _out in (("w1", DM, HID), ("w2", DM, HID), ("h1", HID, HID), ("h2", HID, HID), ("w3", HID, DM)):
    FFN_W[_name] = (FFN_COLS, _in // 128, _out)
    FFN_COLS += _in // 128 * _out
EPS = 1e-5
GT = 512
TPG = GT // P
GROUPS = TOK // GT
QG = SEQ // GT
KT = SEQ // P
VW = LAT + 1
VPARTS = 3
VC = VPARTS * VW
SROWS = 3 * LAT
SCALE = float(HD) ** -0.5
NEG = -1e30
PSHIFT = 14.0 * float(np.log(2.0))


STORES = KV + 3


class Chain:

    def __init__(self, eng, sem, base=0):
        self.eng, self.sem, self.base, self.n = eng, sem, base, 0

    def __call__(self, ins):
        self.n += 1
        ins.then_inc(self.sem, 1)
        self.eng.wait_ge(self.sem, self.base + self.n)


def layer(nc, x, wqT, wkd, wvd, wkuT, wvuT, wo, ffn_w, s1, s2, sh1, sh2, s3, out):
    q_dram = nc.dram_tensor("q_parts", [2, HEADS * LAT, TOK], F32, kind="Internal").ap()
    k_dram = nc.dram_tensor("k_parts", [2, KV * LAT, TOK], F32, kind="Internal").ap()
    v_dram = nc.dram_tensor("v_parts", [P, KV, TOK // P, VC], BF16, kind="Internal").ap()
    with ExitStack() as keep:
        sb = lambda name, shape, dt: keep.enter_context(nc.sbuf_tensor(name, shape, dt))
        W = {}
        W["ident"] = sb("ident", [P, P], F32)
        W["identb"] = sb("identb", [P, P], BF16)
        W["mhalf"] = sb("mhalf", [P, TPG], F32)
        W["eps"] = sb("eps", [P, TPG], F32)
        W["wo_eff"] = sb("wo_eff", [P, KV, DM], F32)
        W["w_hi"] = sb("ffn_w_hi", [P, FFN_COLS], F32R)
        W["w_lo"] = sb("ffn_w_lo", [P, FFN_COLS], F32R)
        W["w_cut"] = sb("ffn_w_cut", [P, FFN_COLS // HEADS], BF16)
        W["ones"] = sb("ones", [P, 1], F32)
        W["x"] = sb("x_all", [P, TOK // P, DM], F32)
        W["s1"], W["s2"], W["sh1"], W["sh2"] = (sb("scale_" + n, [P, 4], F32) for n in ("w1", "w2", "h1", "h2"))
        W["s3"] = sb("scale_w3", [P, 1], F32)
        W["y"] = sb("y_lat", [P, BATCH * KT, HEADS * LAT], F32)
        ql = sb("ql", [P, KV, TOK], F32R)
        W["ys"] = [ql[:, 0, u * TPG * HEADS * LAT:(u + 1) * TPG * HEADS * LAT].bitcast(F32)
                   .rearrange("p (t l) -> p t l", t=TPG) for u in range(2)]
        W["y_loaded"] = [keep.enter_context(nc.semaphore(f"y_loaded{u}")) for u in range(2)]
        with ExitStack() as stay:
            sa = lambda name, shape, dt: stay.enter_context(nc.sbuf_tensor(name, shape, dt))
            A = {}
            A["qs"] = [sa(f"qs{e}", [P, SEQ], F32R) for e in range(BATCH)]
            A["ks"] = [sa(f"ks{e}", [P, SEQ], F32R) for e in range(BATCH)]
            A["vs"] = [sa(f"vs{e}", [P, KT, VC], BF16) for e in range(BATCH)]
            A["mask_q"] = sa("mask_q", [P, P], BF16)
            A["mask_k"] = sa("mask_k", [P, P], BF16)
            A["shift"] = sa("shift", [P, 1], F32)
            A["mcols"] = sa("mcols", [P, TPG, P], BF16)
            A["ql"] = ql
            for name in ("qk_loaded", "v_loaded", "latents_stored"):
                A[name] = [stay.enter_context(nc.semaphore(f"{name}{n}")) for n in range(2)]
            prepare(nc, W, A, x, wqT, wkd, wvd, wkuT, wvuT, wo, ffn_w, s1, s2, sh1, sh2, s3,
                    q_dram, k_dram, v_dram)
            attend(nc, W, A, ffn_w, q_dram, k_dram, v_dram)
        finish(nc, W, out)


def load_qk(sp, A, q_dram, k_dram, h, e):
    tok = slice(e * SEQ, (e + 1) * SEQ)
    for n in range(2):
        sp.dma_start(A["qs"][e][n * LAT:(n + 1) * LAT, :].bitcast(F32),
                     q_dram[0, ds(h * LAT, LAT), tok]).then_inc(A["qk_loaded"][e], 16)
    first = isinstance(h, int) and h == 0
    low = A["ql"][0:LAT, 0, tok].bitcast(F32) if first else q_dram[1, ds(h * LAT, LAT), tok]
    sp.dma_start(A["qs"][e][2 * LAT:3 * LAT, :].bitcast(F32), low).then_inc(A["qk_loaded"][e], 16)
    for n, part in enumerate((0, 1, 0)):
        sp.dma_start(A["ks"][e][n * LAT:(n + 1) * LAT, :].bitcast(F32),
                     k_dram[part, ds(h // REP * LAT, LAT), tok]).then_inc(A["qk_loaded"][e], 16)


def load_v(sp, A, v_dram, h, e):
    sp.dma_start(A["vs"][e][:, :, :], v_dram[:, ds(h // REP, 1), e * KT:(e + 1) * KT, :]
                 .rearrange("p o t c -> p (o t) c")).then_inc(A["v_loaded"][e], 16)


def load_y(sp, W, j, u):
    sp.dma_start(W["ys"][u][:, :, :], W["y"][:, ds(j % GROUPS * TPG, TPG), :]).then_inc(W["y_loaded"][u], 16)


def prepare(nc, W, A, x, wqT, wkd, wvd, wkuT, wvuT, wo, ffn_w, s1, s2, sh1, sh2, s3,
            q_dram, k_dram, v_dram):
    with ExitStack() as ctx:
        sb = lambda name, shape, dt: ctx.enter_context(nc.sbuf_tensor(name, shape, dt))
        sem = lambda name: ctx.enter_context(nc.semaphore(name))
        psum = lambda name, shape: ctx.enter_context(nc.psum_tensor(name, shape, F32))
        half = HEADS * DM // (HEADS * LAT)
        wq_sb, wo_sb = (W["y"][:, n * half:(n + 1) * half, :].rearrange("p a (b m) -> p (a b) m", m=DM)
                        for n in range(2))
        wku = sb("wku", [P, LAT], F32)
        wvu_pad = sb("wvu_pad", [P, REP, REP, LAT], F32)
        wkd_sb = sb("wkd_sb", [P, KV * LAT], F32)
        wvd_sb = sb("wvd_sb", [P, KV * LAT], F32)
        q_w = sb("q_w", [P, KV, P], F32)
        bst = [sb(f"bst{u}", [P, TPG, 6], F32) for u in range(2)]
        mv = [sb(f"mv{u}", [P, TPG, 2], F32) for u in range(2)]
        ve = [sb(f"ve{u}", [P, TPG], F32) for u in range(2)]
        rstd = [sb(f"rstd{u}", [P, TPG], F32) for u in range(2)]
        rows = GT // (HEADS * LAT)
        spare = [W["y"][:, 2 * half + n * rows:2 * half + (n + 1) * rows, :] for n in range(4)]
        xn = [a.rearrange("p a (b d) -> p (a b) d", d=DM) for a in spare[:2]]
        xnT = [a.rearrange("p a b -> p (a b)") for a in spare[2:]]
        qh = [sb(f"qh{u}", [P, KV, GT], F32R) for u in range(2)]
        kh = [sb(f"kh{u}", [KV * LAT, GT], F32R) for u in range(2)]
        kl = [sb(f"kl{u}", [KV * LAT, GT], F32R) for u in range(2)]
        vp = [sb(f"vp{u}", [P, KV, TPG, VC], BF16) for u in range(2)]
        vf = [sb(f"vf{u}", [P, KV, TPG, LAT], F32) for u in range(2)]
        zeros = sb("zeros", [P, KV, TPG, LAT], F32)
        held = sb("held", [P, 1], F32)
        psT = [psum(f"psT{u}", [P, GT]) for u in range(2)]
        psK = psum("psK", [P, GT])
        psQ = [psum(f"psQ{c}", [P, GT]) for c in range(KV)]
        psV = psum("psV", [P, TPG, KV * LAT])
        psA = psum("psA", [P, KV, P])
        psW = psum("psW", [P, KV, P])

        w_loaded = sem("w_loaded")
        ffn_loaded = sem("ffn_loaded")
        consts = sem("consts")
        x_loaded = [sem(f"x_loaded{n}") for n in range(2)]
        mv_ready = sem("mv_ready")
        rstd_ready = sem("rstd_ready")
        xn_ready = sem("xn_ready")
        t_ready = sem("t_ready")
        xnT_ready = sem("xnT_ready")
        proj_ready = sem("proj_ready")
        w_ready = sem("w_ready")
        qw_ready = sem("qw_ready")
        hi_ready = sem("hi_ready")
        lo_ready = sem("lo_ready")
        v_ready = sem("v_ready")
        vf_ready = sem("vf_ready")
        stored = A["latents_stored"]
        d1 = sem("dve_chain")
        d2 = sem("dve_ones")
        p1 = sem("pool_chain")
        v_chain = sem("v_chain")
        mask_chain = sem("mask_chain")

        X_CUTS = (0, 2 * TPG, TOK // P)

        def load_x(sp, n):
            a, b = X_CUTS[n], X_CUTS[n + 1]
            sp.dma_start(W["x"][:, a:b, :], x[a * P:b * P, :].rearrange("(t p) d -> p t d", p=P))\
              .then_inc(x_loaded[n], 16)

        with nc.Block() as block:

            @block.sync
            def _(sp):
                load_x(sp, 0)
                sp.dma_start(wq_sb[:, :, :], wqT.rearrange("(h d) m -> d h m", d=HD)).then_inc(w_loaded, 16)
                sp.dma_start(wku[:, :], wkuT).then_inc(w_loaded, 16)
                sp.dma_start(wkd_sb[:, :], wkd).then_inc(w_loaded, 16)
                sp.dma_start(wvd_sb[:, :], wvd).then_inc(w_loaded, 16)
                sp.dma_start(wo_sb[:, :, :], wo.rearrange("(h d) m -> d h m", d=HD)).then_inc(w_loaded, 16)
                sp.wait_ge(consts, 1)
                for r in range(REP):
                    sp.dma_start(wvu_pad[:, r, r, :], wvuT).then_inc(w_loaded, 16)
                load_x(sp, 1)
                for n, s in (("s1", s1), ("s2", s2), ("sh1", sh1), ("sh2", sh2), ("s3", s3)):
                    sp.dma_start(W[n][:, :], s).then_inc(ffn_loaded, 16)
                for e in range(BATCH):
                    with sp.Fori(e * QG // 2, (e + 1) * QG // 2) as i:
                        for u in range(2):
                            tok = ds(sp.snap((2 * i + u) * GT), GT)
                            tiles = ds(sp.snap((2 * i + u) * TPG), TPG)
                            sp.wait_ge(lo_ready, 3 * (2 * i + u + 2))
                            for c in range(KV):
                                sp.dma_start(q_dram[0, c * P:(c + 1) * P, tok], qh[u][:, c, :].bitcast(F32))\
                                  .then_inc(stored[u], 16)
                            sp.dma_start(k_dram[0, :, tok], kh[u][:, :].bitcast(F32)).then_inc(stored[u], 16)
                            sp.dma_start(k_dram[1, :, tok], kl[u][:, :].bitcast(F32)).then_inc(stored[u], 16)
                            sp.wait_ge(v_ready, 2 * i + u + 1)
                            sp.dma_start(v_dram[:, :, tiles, :], vp[u][:, :, :, :]).then_inc(stored[u], 16)
                    if e == 0:
                        for u in range(2):
                            sp.wait_ge(stored[u], STORES * 16 * (QG // 2 + 1))
                        sp.wait_ge(lo_ready, 3 * (QG + 1))
                        load_qk(sp, A, q_dram, k_dram, 0, 0)
                        load_v(sp, A, v_dram, 0, 0)
                sp.wait_ge(ffn_loaded, 16 * 5)

            @block.gpsimd
            def _(pool):
                pool.memset(wvu_pad[:, :, :, :], 0.0).then_inc(consts, 1)
                pool.memset(W["mhalf"][:, :], -0.5)
                pool.memset(W["eps"][:, :], EPS)
                pool.memset(W["ones"][:, :], 1.0)
                pool.memset(W["w_cut"][:, :], 0.0)
                pool.memset(zeros[:, :, :, :], 0.0)
                pool.memset(W["ident"][:, :], 0.0).then_inc(p1, 1)
                pool.wait_ge(p1, 1)
                pool.affine_select(out=W["ident"][:, :], in_=W["ident"][:, :], compare_op=ALU.not_equal, fill=1.0,
                                   base=0, pattern=[[-1, P]], channel_multiplier=1).then_inc(p1, 1)
                pool.wait_ge(p1, 2)
                pool.tensor_copy(W["identb"][:, :], W["ident"][:, :]).then_inc(consts, 1)

                link = Chain(pool, mask_chain)
                link(pool.memset(A["mask_q"][:, :], 0.0))
                link(pool.affine_select(out=A["mask_q"][:, :], in_=A["mask_q"][:, :], compare_op=ALU.is_ge, fill=NEG,
                                        base=0, pattern=[[-1, P]], channel_multiplier=1))
                link(pool.memset(A["mask_k"][:, :], 0.0))
                link(pool.affine_select(out=A["mask_k"][:, :], in_=A["mask_k"][:, :], compare_op=ALU.is_ge, fill=NEG,
                                        base=0, pattern=[[1, P]], channel_multiplier=-1))

                def rstd_of(j, u):
                    pool.wait_ge(mv_ready, j + 1)
                    pool.tensor_tensor(ve[u][:, :], mv[u][:, :, 1], W["eps"][:, :], ALU.add).then_inc(p1, 1)
                    pool.wait_ge(p1, 2 + j + 1)
                    pool.tensor_tensor(rstd[u][:, :], ve[u][:, :], W["mhalf"][:, :], ALU.pow).then_inc(rstd_ready, 1)

                rstd_of(0, 0)
                rstd_of(1, 1)
                with pool.Fori(0, GROUPS // 2) as i:
                    for u in range(2):
                        j = 2 * i + u
                        rstd_of(j + 2, u)
                        pool.wait_ge(vf_ready, 1 + j + 1)
                        v = vf[u][:, :, :, :]
                        part = [vp[u][:, :, :, VW * n:VW * n + LAT] for n in range(VPARTS)]
                        link = Chain(pool, v_chain, 2 * j)
                        link(pool.tensor_tensor(v, v, part[0], ALU.subtract))
                        link(pool.tensor_tensor(part[1], v, zeros[:, :, :, :], ALU.add))
                        pool.tensor_tensor(part[2], v, part[1], ALU.subtract).then_inc(v_ready, 1)

            @block.scalar
            def _(act):
                act.sem_inc(vf_ready, 1)
                act.wait_ge(qw_ready, 1)
                act.activation(q_w[:, :, :], psA[:, :, :], ACT.Copy).then_inc(w_ready, 1)
                act.wait_ge(qw_ready, 2)
                act.activation(W["wo_eff"][:, :, :], psW[:, :, :], ACT.Copy).then_inc(w_ready, 1)

                def xnT_out(j, u):
                    act.wait_ge(t_ready, j + 1)
                    act.activation(xnT[u][:, :], psT[u][:, :], ACT.Copy).then_inc(xnT_ready, 1)

                xnT_out(0, 0)
                with act.Fori(0, GROUPS // 2) as i:
                    for u in range(2):
                        j = 2 * i + u
                        act.wait_ge(stored[u], STORES * 16 * (i + 1))
                        act.wait_ge(proj_ready, 4 * j + 1)
                        act.activation(kh[u][:, :], psK[0:KV * LAT, :], ACT.Copy).then_inc(hi_ready, 1)
                        xnT_out(j + 1, 1 - u)
                        for c in range(KV):
                            act.wait_ge(proj_ready, 4 * j + 2 + c)
                            act.activation(qh[u][:, c, :], psQ[c][:, :], ACT.Copy).then_inc(hi_ready, 1)
                        act.wait_ge(proj_ready, 4 * j + 4)
                        v = psV[:, :, :].rearrange("p t (c l) -> p c t l", c=KV)
                        act.activation(vf[u][:, :, :, :], v, ACT.Copy)
                        act.activation(vp[u][:, :, :, 0:LAT], v, ACT.Copy).then_inc(vf_ready, 1)

            @block.vector
            def _(dve):
                for u in range(2):
                    dve.memset(vp[u][:, :, :, :], 0.0).then_inc(d1, 1)
                dve.wait_ge(d1, 2)
                for u in range(2):
                    dve.memset(vp[u][:, :, :, LAT:LAT + 1], 1.0).then_inc(d1, 1)
                dve.wait_ge(d1, 4)
                for u in range(2):
                    dve.sem_inc(stored[u], STORES * 16)
                dve.sem_inc(lo_ready, 3)

                def x_tile(j, t):
                    return W["x"][:, ds(j % GROUPS * TPG + t, 1), :].rearrange("p o d -> p (o d)")

                def moments(j, u):
                    for t in range(TPG):
                        last = dve.bn_stats(bst[u][:, t, :], x_tile(j, t))
                    last.then_inc(d1, 1)
                    dve.wait_ge(d1, 4 + j + 1)
                    dve.memset(held[:, :], 0.0)
                    for t in range(TPG):
                        last = dve.bn_aggr(mv[u][:, t, :], bst[u][:, t, :])
                    last.then_inc(mv_ready, 1)

                def normalise(j, u):
                    dve.wait_ge(mv_ready, j + 1)
                    dve.wait_ge(rstd_ready, j + 1)
                    for t in range(TPG):
                        last = dve.tensor_scalar(xn[u][:, t, :], x_tile(j, t), mv[u][:, t, 0:1],
                                                 rstd[u][:, t:t + 1], ALU.subtract, ALU.mult)
                    last.then_inc(xn_ready, 1)

                for e in range(BATCH):
                    dve.memset(A["ks"][e][SROWS:P, :].bitcast(F32), 0.0).then_inc(d2, 1)
                dve.memset(A["mcols"][:, :, :], 0.0)
                dve.memset(A["shift"][:, :], PSHIFT)
                dve.wait_ge(d2, BATCH)
                for e in range(BATCH):
                    dve.memset(A["ks"][e][SROWS:SROWS + 2, :].bitcast(F32), 1.0)
                dve.wait_ge(x_loaded[0], 16)
                for j in range(2):
                    moments(j, j)
                for j in range(2):
                    normalise(j, j)
                dve.wait_ge(x_loaded[1], 16)
                with dve.Fori(0, GROUPS // 2) as i:
                    for u in range(2):
                        j = 2 * i + u
                        moments(j + 2, u)
                        dve.wait_ge(hi_ready, 3 * j + 1)
                        dve.tensor_tensor(kl[u][:, :], psK[0:KV * LAT, :], kh[u][:, :].bitcast(F32), ALU.subtract)\
                           .then_inc(lo_ready, 1)
                        for c in range(KV):
                            dve.wait_ge(hi_ready, 3 * j + 2 + c)
                            dve.tensor_tensor(A["ql"][:, c, ds(j * GT, GT)], psQ[c][:, :], qh[u][:, c, :].bitcast(F32),
                                              ALU.subtract).then_inc(lo_ready, 1)
                            if c == 0:
                                dve.wait_ge(t_ready, j + 1)
                                normalise(j + 2, u)

            @block.tensor
            def _(pe):
                pe.wait_ge(w_loaded, 16 * 9)
                for h in range(HEADS):
                    c, r = divmod(h, REP)
                    last = pe.matmul(psA[:, c, r * LAT:(r + 1) * LAT], wq_sb[:, h, :], wku[:, :],
                                     start=True, stop=True)
                last.then_inc(qw_ready, 1)
                for c in range(KV):
                    for r in range(REP):
                        last = pe.matmul(psW[:, c, :], wvu_pad[:, r, :, :].rearrange("p a l -> p (a l)"),
                                         wo_sb[:, c * REP + r, :], start=(r == 0), stop=(r == REP - 1))
                last.then_inc(qw_ready, 1)
                pe.wait_ge(consts, 2)
                pe.wait_ge(w_ready, 1)

                def turn(j, u):
                    pe.wait_ge(xn_ready, j + 1)
                    for t in range(TPG):
                        last = pe.transpose(psT[u][:, t * P:(t + 1) * P], xn[u][:, t, :], W["ident"][:, :])
                    last.then_inc(t_ready, 1)

                turn(0, 0)
                with pe.Fori(0, GROUPS // 2) as i:
                    for u in range(2):
                        j = 2 * i + u
                        pe.wait_ge(xnT_ready, j + 1)
                        pe.wait_ge(lo_ready, 3 * j + 1)
                        pe.matmul(psK[0:KV * LAT, :], wkd_sb[:, :], xnT[u][:, :], start=True, stop=True)\
                          .then_inc(proj_ready, 1)
                        turn(j + 1, 1 - u)
                        for c in range(KV):
                            pe.wait_ge(lo_ready, 3 * j + 2 + c)
                            pe.matmul(psQ[c][:, :], q_w[:, c, :], xnT[u][:, :], start=True, stop=True)\
                              .then_inc(proj_ready, 1)
                        pe.wait_ge(vf_ready, j + 1)
                        for t in range(TPG):
                            last = pe.matmul(psV[:, t, :], xnT[u][:, t * P:(t + 1) * P], wvd_sb[:, :],
                                             start=True, stop=True)
                        last.then_inc(proj_ready, 1)


LAG = 3
NP_BUF = 5
JOBS = BATCH * QG
LEAD = 28
TURN = 2
POOL_SHARE = 0.84


class Pair:

    def __init__(self, job, first):
        self.job, self.e, self.g = job, job // QG, job % QG
        self.tiles, at = [], 0
        for kt in (first, first + 1):
            q0 = max(0, kt - TPG * self.g) * P
            self.tiles.append((kt, q0, at, kt >= TPG * self.g))
            at += GT - q0
        self.width = at
        self.first = first == 0
        self.last = first + 2 == TPG * (self.g + 1)


PAIRS = [Pair(job, first) for job in range(JOBS) for first in range(0, TPG * (job % QG + 1), 2)]
STEPS = len(PAIRS)
TAIL = STEPS
CHUNKS = [(job, t, c, GT if c < job % QG else (t + 1) * P)
          for job in range(JOBS) for t in range(TPG) for c in range(job % QG + 1)]
NCH = len(CHUNKS)
SHARE = [[LEAD + n for n in range(NCH) if min(n // 2, STEPS) == p or (p == TAIL and n // 2 == STEPS - 1)]
         for p in range(STEPS + 1)]
SHARE[STEPS - 1] = []


def ends_job(n):
    return n % NCH == NCH - 1 or CHUNKS[(n + 1) % NCH][0] != CHUNKS[n % NCH][0]


TURNS = [[(n // NCH, CHUNKS[n % NCH][0]) for p in range(STEPS + 1) for n in SHARE[p]
          if ends_job(n) and min(p + TURN, TAIL) == step] for step in range(STEPS + 1)]
PRE_TURNS = [CHUNKS[n][0] for n in range(LEAD) if ends_job(n)]
for _step, _turns in enumerate(TURNS):
    for _ahead, _job in _turns:
        assert _step < _ahead * STEPS + min(p for p in range(STEPS) if PAIRS[p].job == _job) - LAG


def rest_columns(k):
    width = PAIRS[k % STEPS].width
    cut = int(width * POOL_SHARE) // 64 * 64
    return slice(0, cut), slice(cut, width)


def ended(p):
    return PAIRS[p].job if 0 <= p < STEPS and PAIRS[p].last else None


def attend(nc, W, A, ffn_w, q_dram, k_dram, v_dram):
    with ExitStack() as ctx:
        sb = lambda name, shape, dt: ctx.enter_context(nc.sbuf_tensor(name, shape, dt))
        sem = lambda name: ctx.enter_context(nc.semaphore("a_" + name))
        psum = lambda name, shape: ctx.enter_context(nc.psum_tensor(name, shape, F32))
        qs, ks, vs, mask_q, mask_k, shift, mcols = (A[n] for n in ("qs", "ks", "vs", "mask_q", "mask_k", "shift",
                                                                   "mcols"))
        qk_loaded, v_loaded = A["qk_loaded"], A["v_loaded"]
        mpart = [sb(f"mpart{n}", [P, TPG, QG], F32) for n in range(2)]
        nmax = sb("nmax", [P, TPG], F32)
        sums = sb("sums", [P, TPG, VW], F32)
        rden = sb("rden", [P, TPG], F32)
        w_raw = sb("ffn_w_raw", [P, FFN_COLS // HEADS], F32)
        acc_sb = [sb(f"acc_sb{n}", [VC, GT], F32) for n in range(2)]
        prob = [sb(f"prob{n}", [P, 2 * GT], F32) for n in range(NP_BUF)]
        rest = [sb(f"rest{n}", [P, 2 * GT], F16) for n in range(NP_BUF)]
        s_max = [psum(f"s_max{n}", [P, GT]) for n in range(2)]
        s_t = [psum(f"s_t{n}", [P, 2 * GT]) for n in range(2)]
        acc = [psum(f"acc{n}", [P, GT]) for n in range(2)]
        turned_sums = [acc[n][:, :].rearrange("p (t q) -> p t q", q=P) for n in range(2)]
        turned_max = [acc[n][:, :].bitcast(BF16)[:, 0:GT] for n in range(2)]

        w_loaded, lows_stored = sem("w_loaded"), sem("lows_stored")
        w_hi_ready, w_lo_ready, cut_noted = sem("w_hi_ready"), sem("w_lo_ready"), sem("cut_noted")
        smax_ready = sem("smax_ready")
        max_done = sem("max_done")
        nmax_chain = sem("nmax_chain")
        nmax_ready = sem("nmax_ready")
        turn_ready = sem("turn_ready")
        mrow_ready = sem("mrow_ready")
        st_ready = sem("st_ready")
        exp_done = sem("exp_done")
        rest_pool = sem("rest_pool")
        rest_dve = sem("rest_dve")
        pv_done = sem("pv_done")
        acc_copied = sem("acc_copied")
        sums_ready = sem("sums_ready")
        y_chain = sem("y_chain")
        y_read = sem("y_read")
        y_done = sem("y_done")
        FREE_MAX, FREE_ST, FREE_P, FREE_Y, FREE_SUMS = 2, 2, NP_BUF, 2, 1

        def turns(p, h, last):
            return [(job, (h + ahead) * JOBS + job) for ahead, job in TURNS[p] if not (ahead and last)]

        def share(p, last):
            return [n for n in SHARE[p] if not (last and n >= NCH)]

        def other_bank(p):
            return 1 - PAIRS[p].job % 2

        def pair_at(k, last):
            return None if last and k >= STEPS else k

        def heads(body):
            def run(eng):
                with eng.Fori(0, HEADS - 1) as h:
                    body(h, False)
                body(HEADS - 1, True)
            return run

        def take_rest(eng, k, number, columns, done):
            n = k % NP_BUF
            eng.wait_ge(exp_done, FREE_ST + number + 1)
            eng.tensor_tensor(rest[n][:, columns], prob[n][:, columns],
                              prob[n][:, :].bitcast(BF16)[:, 1::2][:, columns], ALU.subtract).then_inc(done, 1)

        with nc.Block() as block:

            @block.sync
            def _(sp):
                def load_w(h):
                    sp.dma_start(w_raw[:, :], ffn_w[:, ds(h * (FFN_COLS // HEADS), FFN_COLS // HEADS)])\
                      .then_inc(w_loaded, 16)

                for u in range(2):
                    sp.wait_ge(A["latents_stored"][u], STORES * 16 * (GROUPS // 2 + 1))
                load_qk(sp, A, q_dram, k_dram, 0, 1)
                load_v(sp, A, v_dram, 0, 1)
                load_w(0)
                for c in range(KV):
                    sp.dma_start(q_dram[1, c * P:(c + 1) * P, :], A["ql"][:, c, :].bitcast(F32))\
                      .then_inc(lows_stored, 16)
                sp.wait_ge(lows_stored, KV * 16)
                with sp.Fori(0, HEADS - 1) as h:
                    sp.wait_ge(w_lo_ready, h + 1)
                    load_w(h + 1)
                    for e in range(BATCH):
                        sp.wait_ge(st_ready, h * STEPS + STEPS // BATCH * (e + 1))
                        load_qk(sp, A, q_dram, k_dram, h + 1, e)
                        sp.wait_ge(pv_done, FREE_P + h * STEPS + STEPS // BATCH * (e + 1))
                        load_v(sp, A, v_dram, h + 1, e)
                for j in range(2):
                    sp.wait_ge(y_chain, FREE_SUMS + 2 * ((HEADS - 1) * JOBS + j + 1))
                    load_y(sp, W, j, j)

            @block.gpsimd
            def _(pool):
                for k in range(LAG):
                    take_rest(pool, k, k, rest_columns(k)[0], rest_pool)

                def body(h, last):
                    for p in range(STEPS):
                        k = pair_at(p + LAG, last)
                        if k is not None:
                            take_rest(pool, k, h * STEPS + k, rest_columns(k)[0], rest_pool)
                        if p == 2:
                            pool.wait_ge(w_hi_ready, h + 1)
                            part = ds(h * (FFN_COLS // HEADS), FFN_COLS // HEADS)
                            pool.tensor_tensor(W["w_lo"][:, part], w_raw[:, :],
                                               W["w_hi"][:, part].bitcast(F32), ALU.subtract)\
                                .then_inc(w_lo_ready, 1)
                heads(body)(pool)

            @block.scalar
            def _(act):
                act.sem_inc(exp_done, FREE_ST)

                def mrow(job, number, bank):
                    e, g = divmod(job, QG)
                    act.wait_ge(turn_ready, number + 1)
                    act.activation(qs[e][SROWS:P, g * GT:(g + 1) * GT], turned_max[bank][SROWS:P, :],
                                   ACT.Copy)\
                       .then_inc(mrow_ready, 1)

                def acc_out(p, h):
                    n = ended(p) % 2
                    act.wait_ge(pv_done, FREE_P + h * STEPS + p + 1)
                    act.activation(acc_sb[n][:, :], acc[n][0:VC, :], ACT.Copy).then_inc(acc_copied, 1)

                def exponentials(k, number):
                    width = PAIRS[k % STEPS].width
                    act.wait_ge(st_ready, number + 1)
                    act.wait_ge(pv_done, number + 1)
                    act.activation(prob[k % NP_BUF][:, 0:width], s_t[k % 2][:, 0:width], ACT.Exp,
                                   bias=shift[:, 0:1], scale=SCALE).then_inc(exp_done, 1)

                def body(h, last):
                    for p in range(STEPS + 1):
                        if p == STEPS - 1:
                            acc_out(p, h)
                        if p < STEPS and (k := pair_at(p + LAG, last)) is not None:
                            exponentials(k, h * STEPS + k)
                        for job, number in turns(p, h, last):
                            mrow(job, number, other_bank(p))
                        if p < STEPS - 1 and ended(p) is not None:
                            acc_out(p, h)
                        if p == 0:
                            part = ds(h * (FFN_COLS // HEADS), FFN_COLS // HEADS)
                            act.wait_ge(w_loaded, 16 * (h + 1))
                            act.activation(W["w_hi"][:, part], w_raw[:, :], ACT.Copy)\
                               .then_inc(w_hi_ready, 1)

                for job in PRE_TURNS:
                    mrow(job, job, 1)
                for u in range(2):
                    act.wait_ge(A["latents_stored"][u], STORES * 16 * (GROUPS // 2 + 1))
                for k in range(LAG):
                    exponentials(k, k)
                heads(body)(act)

            @block.vector
            def _(dve):
                dve.sem_inc(max_done, FREE_MAX)
                dve.sem_inc(y_read, FREE_Y)
                dve.sem_inc(y_chain, FREE_SUMS)

                def maximum(n, h):
                    job, t, c, width = CHUNKS[n % NCH]
                    dve.wait_ge(smax_ready, h * NCH + n + 1)
                    dve.reduce_max(mpart[job % 2][:, t, c:c + 1], s_max[n % 2][:, 0:width], AX.X)\
                       .then_inc(max_done, 1)

                def nmax_reduce(n, h):
                    job, jn = CHUNKS[n % NCH][0], (h + n // NCH) * JOBS + CHUNKS[n % NCH][0]
                    dve.wait_ge(max_done, FREE_MAX + h * NCH + n + 1)
                    dve.tensor_reduce(nmax[:, :], mpart[job % 2][:, :, 0:job % QG + 1], AX.X, ALU.max,
                                      negate=True).then_inc(nmax_chain, 1)

                def nmax_high(n, h):
                    jn = (h + n // NCH) * JOBS + CHUNKS[n % NCH][0]
                    if not (isinstance(jn, int) and jn == 0):
                        dve.wait_ge(turn_ready, jn)
                    dve.wait_ge(nmax_chain, 2 * jn + 1)
                    dve.tensor_copy(mcols[:, :, SROWS], nmax[:, :]).then_inc(nmax_chain, 1)

                def nmax_low(n, h):
                    jn = (h + n // NCH) * JOBS + CHUNKS[n % NCH][0]
                    dve.wait_ge(nmax_chain, 2 * jn + 2)
                    dve.tensor_tensor(mcols[:, :, SROWS + 1], nmax[:, :], mcols[:, :, SROWS], ALU.subtract)\
                       .then_inc(nmax_ready, 1)

                def weigh_sum(job, h):
                    dve.wait_ge(y_chain, FREE_SUMS + 2 * (h * JOBS + job))
                    dve.wait_ge(sums_ready, h * JOBS + job + 1)
                    dve.tensor_reduce(sums[:, :, :], turned_sums[job % 2][:, :, 0:VC].rearrange("p t (n c) -> p t c n", n=VPARTS),
                                      AX.X, ALU.add).then_inc(y_read, 1)

                def weigh_denominator(job, h):
                    dve.wait_ge(y_read, FREE_Y + h * JOBS + job + 1)
                    dve.reciprocal(rden[:, :], sums[:, :, LAT]).then_inc(y_chain, 1)

                def weigh_divide(job, h):
                    e, g = divmod(job, QG)
                    dve.wait_ge(y_chain, FREE_SUMS + 2 * (h * JOBS + job) + 1)
                    dve.tensor_tensor(W["y"][:, e * KT + g * TPG:e * KT + (g + 1) * TPG, ds(h * LAT, LAT)],
                                      sums[:, :, 0:LAT], rden[:, :].unsqueeze(2).to_broadcast([P, TPG, LAT]),
                                      ALU.mult).then_inc(y_chain, 1)

                def last_chunks(p, last):
                    return [n for n in share(p, last) if ends_job(n)] if p >= 0 else []

                def body(h, last):
                    for p in range(STEPS + 1):
                        chunks, maxed = share(p, last), last_chunks(p - 1, last)
                        for n in chunks[:1]:
                            maximum(n, h)
                        for n in maxed:
                            nmax_high(n, h)
                        if (job := ended(p - 3)) is not None:
                            weigh_divide(job, h)
                        if p < TAIL and (job := ended(p - 2)) is not None:
                            weigh_sum(job, h)
                        for n in chunks[1:]:
                            maximum(n, h)
                        for n in maxed:
                            nmax_low(n, h)
                        if p < STEPS:
                            k = pair_at(p + LAG - 1, last)
                            if k is not None:
                                take_rest(dve, k, h * STEPS + k, rest_columns(k)[1], rest_dve)
                        if p < TAIL and (job := ended(p - 2)) is not None:
                            weigh_denominator(job, h)
                        for n in last_chunks(p, last):
                            nmax_reduce(n, h)
                            if p == TAIL:
                                nmax_high(n, h)
                                nmax_low(n, h)
                        if p == TAIL:
                            job = ended(p - 1)
                            weigh_sum(job, h)
                            weigh_denominator(job, h)
                            weigh_divide(job, h)
                        if p == STEPS // 2:
                            dve.wait_ge(w_lo_ready, h + 1)
                            part = ds(h * (FFN_COLS // HEADS), FFN_COLS // HEADS)
                            dve.scalar_tensor_tensor(out=W["w_cut"][:, :], in0=W["w_lo"][:, part].bitcast(F32),
                                                     scalar=0.0, in1=W["w_cut"][:, :], op0=ALU.not_equal,
                                                     op1=ALU.max).then_inc(cut_noted, 1)

                for n in range(LEAD):
                    maximum(n, 0)
                    if ends_job(n):
                        nmax_reduce(n, 0)
                        nmax_high(n, 0)
                        nmax_low(n, 0)
                for k in range(LAG - 1):
                    take_rest(dve, k, k, rest_columns(k)[1], rest_dve)
                heads(body)(dve)

            @block.tensor
            def _(pe):
                pe.sem_inc(pv_done, FREE_P)

                def scores_q(n, h):
                    job, t, c, width = CHUNKS[n % NCH]
                    e, g = divmod(job, QG)
                    number = h * NCH + n
                    if n % NCH in (0, NCH // BATCH):
                        pe.wait_ge(qk_loaded[e], 6 * 16 * (h + n // NCH + 1))
                    pe.wait_ge(max_done, number + 1)
                    bank = s_max[n % 2]
                    diagonal = c == g
                    q = (g * TPG + t) * P
                    last = pe.matmul(bank[:, 0:width], qs[e][0:SROWS, q:q + P],
                                     ks[e][0:SROWS, c * GT:c * GT + width], start=True, stop=not diagonal)
                    if diagonal:
                        last = pe.matmul(bank[:, width - P:width], W["identb"][:, :], mask_q[:, :],
                                         start=False, stop=True)
                    last.then_inc(smax_ready, 1)

                def scores_k(k, number, h):
                    pair = PAIRS[k % STEPS]
                    if pair.first:
                        pe.wait_ge(mrow_ready, (h + k // STEPS) * JOBS + pair.job + 1)
                    pe.wait_ge(exp_done, number + 1)
                    for kt, q0, at, diagonal in pair.tiles:
                        width = GT - q0
                        last = pe.matmul(s_t[k % 2][:, at:at + width], ks[pair.e][:, kt * P:(kt + 1) * P],
                                         qs[pair.e][:, pair.g * GT + q0:(pair.g + 1) * GT],
                                         start=True, stop=not diagonal)
                        if diagonal:
                            last = pe.matmul(s_t[k % 2][:, at:at + P], W["identb"][:, :], mask_k[:, :],
                                             start=False, stop=True)
                    last.then_inc(st_ready, 1)

                def turn_maxima(number, jobs, bank):
                    pe.wait_ge(nmax_ready, number + 1)
                    pe.wait_ge(y_read, FREE_Y + jobs)
                    if not (isinstance(number, int) and number == 0):
                        pe.wait_ge(mrow_ready, number)
                    for t in range(TPG):
                        last = pe.transpose(turned_max[bank][:, t * P:(t + 1) * P], mcols[:, t, :], W["identb"][:, :])
                    last.then_inc(turn_ready, 1)

                def turn_sums(job, number):
                    pe.wait_ge(acc_copied, number + 1)
                    for t in range(TPG):
                        last = pe.transpose(turned_sums[job % 2][:, t, 0:VC], acc_sb[job % 2][:, t * P:(t + 1) * P],
                                            W["ident"][0:VC, 0:VC])
                    last.then_inc(sums_ready, 1)

                def multiply(p, h, turned):
                    pair = PAIRS[p]
                    if p in (0, STEPS // BATCH):
                        pe.wait_ge(v_loaded[pair.e], 16 * (h + 1))
                    if pair.first:
                        pe.wait_ge(y_read, FREE_Y + h * JOBS + pair.job - 1)
                        pe.wait_ge(mrow_ready, turned)
                    pe.wait_ge(rest_dve, h * STEPS + p + 1)
                    pe.wait_ge(rest_pool, h * STEPS + p + 1)
                    high = prob[p % NP_BUF][:, :].bitcast(BF16)[:, 1::2]
                    for half, (kt, q0, at, _) in enumerate(pair.tiles):
                        v = vs[pair.e][:, kt, :]
                        pe.matmul(acc[pair.job % 2][0:VC, q0:GT], v, high[:, at:at + GT - q0],
                                  start=(pair.first and half == 0), stop=False)
                        last = pe.matmul(acc[pair.job % 2][0:VC, q0:GT], v, rest[p % NP_BUF][:, at:at + GT - q0],
                                         start=False, stop=pair.last and half == 1)
                    last.then_inc(pv_done, 1)

                def body(h, last):
                    turned = len(PRE_TURNS) + h * JOBS
                    for p in range(STEPS + 1):
                        chunks = share(p, last)
                        if p == STEPS - 1:
                            multiply(p, h, turned)
                        if chunks:
                            scores_q(chunks[0], h)
                        if p < STEPS and (k := pair_at(p + LAG, last)) is not None:
                            scores_k(k, h * STEPS + k, h)
                        for n in chunks[1:]:
                            scores_q(n, h)
                        if p < STEPS - 1:
                            multiply(p, h, turned)
                        if (job := ended(p - 1)) is not None:
                            turn_sums(job, h * JOBS + job)
                        for _, number in turns(p, h, last):
                            turn_maxima(number, h * JOBS + PAIRS[p].job, other_bank(p))
                            turned = turned + 1

                for n in range(LEAD + TURN):
                    if n < LEAD:
                        scores_q(n, 0)
                    if n >= TURN and ends_job(n - TURN):
                        turn_maxima(CHUNKS[n - TURN][0], 0, 1)
                for k in range(LAG):
                    scores_k(k, k, 0)
                heads(body)(pe)


def finish(nc, W, out):
    with ExitStack() as ctx:
        sb = lambda name, shape, dt: ctx.enter_context(nc.sbuf_tensor(name, shape, dt))
        sem = lambda name: ctx.enter_context(nc.semaphore("f_" + name))
        psum = lambda name, shape: ctx.enter_context(nc.psum_tensor(name, shape, F32))
        MT = HID // P
        two = range(2)
        ys, y_loaded = W["ys"], W["y_loaded"]
        yT = sb("f_yT", [P, KV, GT], F32)
        stats = {n: sb(f"f_stats_{n}", [P, TPG, 6], F32) for n in "abo"}
        mv = {n: sb(f"f_mv_{n}", [P, TPG, 2], F32) for n in "abo"}
        ve = {n: sb(f"f_ve_{n}", [P, TPG], F32) for n in "abo"}
        rstd = {n: sb(f"f_rstd_{n}", [P, TPG], F32) for n in "abo"}
        nrm = sb("f_nrm", [P, TPG, DM], F32)
        xn = sb("f_xn", [P, TPG, DM], F32)
        xh = sb("f_xh", [P, GT], F32R)
        xl = sb("f_xl", [P, GT], F32R)
        sg = [sb(f"f_sg{n}", [P, GT], F32) for n in two]
        full = sb("f_full", [P, MT, GT], F32)
        hi = [sb(f"f_hi{n}", [P, MT, GT], F32R) for n in two]
        lo = [sb(f"f_lo{n}", [P, MT, GT], F32R) for n in two]
        oT = sb("f_oT", [P, GT], F32)
        on = sb("f_on", [P, TPG, DM], F32)
        res = [sb(f"f_res{u}", [P, TPG, DM], F32) for u in two]
        held = {n: sb("f_held_" + n, [P, 1], F32) for n in "abox"}
        held_p = sb("f_held_p", [P, 1], F32)
        cut = sb("f_cut", [P, 1], F32)
        cut_count = sb("f_cut_count", [1, 1], mybir.dt.int32)
        ring = [psum(f"f_ring{n}", [P, GT]) for n in range(4)]
        psY = psum("f_psY", [P, TPG, P])
        psO = psum("f_psO", [P, TPG, P])
        psX = psum("f_psX", [P, TPG, DM])
        psN = psum("f_psN", [P, GT])
        y_banks = (psY, psO)

        y_turned, yT_ready, ao_ready = sem("y_turned"), sem("yT_ready"), sem("ao_ready")
        st = {n: sem(f"stats_{n}") for n in "abo"}
        mv_ready = {n: sem(f"mv_ready_{n}") for n in "abo"}
        rs = {n: sem(f"rstd_{n}") for n in "abo"}
        pc = {n: sem(f"pool_{n}") for n in "abo"}
        nrm_ready, x1_ready, xn_ready = sem("nrm_ready"), sem("x1_ready"), sem("xn_ready")
        n_turned, xh_ready, xl_ready = sem("n_turned"), sem("xh_ready"), sem("xl_ready")
        in_ready, silu_done, prod_done = sem("in_ready"), sem("silu_done"), sem("prod_done")
        hid_ready, gelu_done, hi_ready = sem("hid_ready"), sem("gelu_done"), sem("hi_ready")
        lo_dve, lo_pool = sem("lo_dve"), sem("lo_pool")
        o_ready, oT_ready, o_turned, on_ready = sem("o_ready"), sem("oT_ready"), sem("o_turned"), sem("on_ready")
        res_ready = sem("res_ready")
        stored = [sem(f"stored{u}") for u in two]
        cut_found, cut_counted, cut_known = sem("cut_found"), sem("cut_counted"), sem("cut_known")
        HIGHS, LOWS_DVE, LOWS_POOL = 3 * MT, MT // 2 + 2 * MT, MT // 2

        def wait_low(eng, j, layer, m):
            if layer == 0 and m < MT // 2:
                eng.wait_ge(lo_pool, LOWS_POOL * j + m + 1)
            elif layer == 0:
                eng.wait_ge(lo_dve, 1 + LOWS_DVE * j + m - MT // 2 + 1)
            else:
                eng.wait_ge(lo_dve, 1 + LOWS_DVE * j + MT // 2 + (layer - 1) * MT + m + 1)

        def groups(eng, body):
            with eng.Fori(0, GROUPS // 2) as i:
                for u in two:
                    body(i, 2 * i + u, u)

        with nc.Block() as block:

            @block.sync
            def _(sp):
                for j in (2, 3):
                    sp.wait_ge(y_turned, KV * (j - 1))
                    load_y(sp, W, j, j % 2)

                def body(i, j, u):
                    sp.wait_ge(y_turned, KV * (j + 3))
                    load_y(sp, W, j + 4, u)
                    sp.wait_ge(res_ready, 1 + j + 1)
                    sp.dma_start(out[ds(j * GT, GT), :].rearrange("(t p) d -> p t d", p=P), res[1 - u][:, :, :])\
                      .then_inc(stored[1 - u], 16)
                groups(sp, body)
                for u in two:
                    sp.wait_ge(y_loaded[u], 16 * (2 + GROUPS // 2))
                sp.wait_ge(stored[0], 16 * (2 + GROUPS // 2))
                sp.wait_ge(stored[1], 16 * (1 + GROUPS // 2))

            @block.gpsimd
            def _(pool):
                pool.sem_inc(stored[0], 32)
                pool.sem_inc(stored[1], 16)

                def rstd_of(n, count):
                    pool.wait_ge(mv_ready[n], count)
                    pool.tensor_tensor(ve[n][:, :], mv[n][:, :, 1], W["eps"][:, :], ALU.add).then_inc(pc[n], 1)
                    pool.wait_ge(pc[n], count)
                    pool.tensor_tensor(rstd[n][:, :], ve[n][:, :], W["mhalf"][:, :], ALU.pow).then_inc(rs[n], 1)

                def carry():
                    pool.tensor_tensor(held_p[:, :], W["ones"][:, :], W["ones"][:, :], ALU.mult)

                def x_group(j):
                    return W["x"][:, ds(j % GROUPS * TPG, TPG), :]

                def add_attention(j):
                    pool.wait_ge(nrm_ready, j + 1)
                    carry()
                    pool.tensor_tensor(x_group(j), x_group(j), nrm[:, :, :], ALU.add).then_inc(x1_ready, 1)

                def add_ffn(j, i, u):
                    pool.wait_ge(on_ready, j + 1)
                    pool.wait_ge(stored[u], 16 * (i + 1))
                    carry()
                    pool.tensor_tensor(res[u][:, :, :], x_group(j + GROUPS - 1), on[:, :, :], ALU.add)\
                        .then_inc(res_ready, 1)

                def low(j, m):
                    pool.wait_ge(hi_ready, HIGHS * j + m + 1)
                    pool.tensor_tensor(lo[0][:, m, :], full[:, m, :], hi[0][:, m, :].bitcast(F32), ALU.subtract)\
                        .then_inc(lo_pool, 1)

                rstd_of("a", 1)
                add_attention(0)
                rstd_of("b", 1)

                def body(i, j, u):
                    low(j, 0)
                    low(j, 1)
                    rstd_of("a", 1 + j + 1)
                    add_attention(j + 1)
                    rstd_of("o", j + 1)
                    rstd_of("b", 1 + j + 1)
                    add_ffn(j, i, u)
                groups(pool, body)
                rstd_of("o", GROUPS + 1)
                add_ffn(GROUPS, GROUPS // 2, 0)

            @block.scalar
            def _(act):
                def y_out(j):
                    for c in range(KV):
                        act.wait_ge(y_turned, KV * j + c + 1)
                        act.activation(yT[:, c, :], y_banks[c][:, :, :].rearrange("p t q -> p (t q)"), ACT.Copy)\
                           .then_inc(yT_ready, 1)

                def n_out(j):
                    act.wait_ge(n_turned, j + 1)
                    act.activation(xh[:, :], psN[:, :], ACT.Copy).then_inc(xh_ready, 1)

                def o_out(j):
                    act.wait_ge(o_ready, j + 1)
                    act.wait_ge(o_turned, j + 1)
                    act.wait_ge(xl_ready, j + 1)
                    act.activation(oT[:, :], psN[:, :], ACT.Copy, scale=W["s3"][:, 0:1]).then_inc(oT_ready, 1)

                y_out(0)
                y_out(1)
                n_out(0)

                def body(i, j, u):
                    def high(m):
                        act.wait_ge(prod_done, MT * j + m + 1)
                        act.activation(hi[0][:, m, :], full[:, m, :], ACT.Copy).then_inc(hi_ready, 1)

                    for m in range(MT):
                        act.wait_ge(in_ready, 2 * (MT * j + m) + 1)
                        if m >= 2:
                            act.wait_ge(prod_done, MT * j + m - 1)
                        act.activation(sg[m % 2][:, :], ring[2 * m % 4][:, :], ACT.Silu, scale=W["s1"][:, m:m + 1])\
                           .then_inc(silu_done, 1)
                        if m >= 1:
                            high(m - 1)
                    high(MT - 1)
                    o_out(j)
                    for layer, scale in ((1, "sh1"), (2, "sh2")):
                        for m in range(MT):
                            act.wait_ge(hid_ready, 2 * MT * j + (layer - 1) * MT + m + 1)
                            s = W[scale][:, m:m + 1]
                            act.activation(hi[layer % 2][:, m, :], ring[m][:, :], ACT.Gelu, scale=s)\
                               .then_inc(hi_ready, 1)
                            wait_low(act, j, layer - 1, m)
                            act.activation(full[:, m, :], ring[m][:, :], ACT.Gelu, scale=s).then_inc(gelu_done, 1)
                            if layer == 2 and m == 1:
                                n_out(j + 1)
                    y_out(j + 2)
                groups(act, body)
                o_out(GROUPS)

            @block.vector
            def _(dve):
                dve.sem_inc(lo_dve, 1)

                def moments(n, count, src):
                    for t in range(TPG):
                        last = dve.bn_stats(stats[n][:, t, :], src(t))
                    last.then_inc(st[n], 1)
                    dve.wait_ge(st[n], count)
                    dve.memset(held[n][:, :], 0.0)
                    for t in range(TPG):
                        last = dve.bn_aggr(mv[n][:, t, :], stats[n][:, t, :])
                    last.then_inc(mv_ready[n], 1)

                def normalise(n, count, dst, src, done):
                    dve.wait_ge(mv_ready[n], count)
                    dve.wait_ge(rs[n], count)
                    for t in range(TPG):
                        last = dve.tensor_scalar(dst[:, t, :], src(t), mv[n][:, t, 0:1],
                                                 rstd[n][:, t:t + 1], ALU.subtract, ALU.mult)
                    last.then_inc(done, 1)

                def attention_moments(j):
                    dve.wait_ge(ao_ready, j + 1)
                    moments("a", j + 1, lambda t: psX[:, t, :])

                def attention_normalise(j):
                    normalise("a", j + 1, nrm, lambda t: psX[:, t, :], nrm_ready)

                def x1_tile(j):
                    return lambda t: W["x"][:, ds(j % GROUPS * TPG + t, 1), :].rearrange("p o d -> p (o d)")

                def x1_moments(j):
                    dve.wait_ge(x1_ready, j + 1)
                    dve.memset(held["x"][:, :], 0.0)
                    moments("b", j + 1, x1_tile(j))

                def x1_normalise(j):
                    normalise("b", j + 1, xn, x1_tile(j), xn_ready)

                def output_moments(j):
                    dve.wait_ge(o_turned, 1 + j + 1)
                    moments("o", j + 1, lambda t: psO[:, t, :])

                def output_normalise(j):
                    normalise("o", j + 1, on, lambda t: psO[:, t, :], on_ready)

                def n_low(j):
                    dve.wait_ge(xh_ready, j + 1)
                    dve.tensor_tensor(xl[:, :], psN[:, :], xh[:, :].bitcast(F32), ALU.subtract).then_inc(xl_ready, 1)

                dve.reduce_max(cut[:, :], W["w_cut"][:, :], AX.X).then_inc(cut_found, 1)
                attention_moments(0)
                dve.wait_ge(cut_counted, 1)
                dve.tensor_copy(cut_count[0:1, 0:1], psN[0:1, 0:1]).then_inc(cut_known, 1)
                attention_normalise(0)
                x1_moments(0)
                x1_normalise(0)
                n_low(0)

                def body(i, j, u):
                    def low(layer, m):
                        dve.wait_ge(hi_ready, HIGHS * j + layer * MT + m + 1)
                        if layer:
                            dve.wait_ge(gelu_done, 2 * MT * j + (layer - 1) * MT + m + 1)
                        dve.tensor_tensor(lo[layer % 2][:, m, :], full[:, m, :], hi[layer % 2][:, m, :].bitcast(F32),
                                          ALU.subtract).then_inc(lo_dve, 1)

                    dve.wait_ge(lo_dve, 1 + LOWS_DVE * j)
                    for m in range(MT):
                        dve.wait_ge(in_ready, 2 * (MT * j + m) + 2)
                        dve.wait_ge(silu_done, MT * j + m + 1)
                        dve.scalar_tensor_tensor(out=full[:, m, :], in0=ring[2 * m % 4 + 1][:, :],
                                                 scalar=W["s2"][:, m:m + 1], in1=sg[m % 2][:, :],
                                                 op0=ALU.mult, op1=ALU.mult).then_inc(prod_done, 1)
                    low(0, 2)
                    low(0, 3)
                    attention_moments(j + 1)
                    attention_normalise(j + 1)
                    low(1, 0)
                    output_moments(j)
                    low(1, 1)
                    x1_moments(j + 1)
                    low(1, 2)
                    output_normalise(j)
                    low(1, 3)
                    x1_normalise(j + 1)
                    low(2, 0)
                    low(2, 1)
                    n_low(j + 1)
                    low(2, 2)
                    low(2, 3)
                groups(dve, body)
                output_moments(GROUPS)
                output_normalise(GROUPS)

            @block.tensor
            def _(pe):
                pe.sem_inc(o_ready, 1)
                pe.sem_inc(o_turned, 1)

                def y_turn(i, u, c):
                    pe.wait_ge(y_loaded[u], 16 * (i + 1))
                    for t in range(TPG):
                        last = pe.transpose(y_banks[c][:, t, :], ys[u][:, t, c * P:(c + 1) * P], W["ident"][:, :])
                    last.then_inc(y_turned, 1)

                def project(j):
                    pe.wait_ge(yT_ready, KV * (j + 1))
                    pe.wait_ge(nrm_ready, j)
                    for t in range(TPG):
                        for c in range(KV):
                            last = pe.matmul(psX[:, t, :], yT[:, c, t * P:(t + 1) * P], W["wo_eff"][:, c, :],
                                             start=(c == 0), stop=(c == KV - 1))
                    last.then_inc(ao_ready, 1)

                def n_turn(j):
                    pe.wait_ge(xn_ready, j + 1)
                    for t in range(TPG):
                        last = pe.transpose(psN[:, t * P:(t + 1) * P], xn[:, t, :], W["ident"][:, :])
                    last.then_inc(n_turned, 1)

                def o_turn(j):
                    pe.wait_ge(oT_ready, j + 1)
                    for t in range(TPG):
                        last = pe.transpose(psO[:, t, :], oT[:, t * P:(t + 1) * P], W["ident"][:, :])
                    last.then_inc(o_turned, 1)

                def feed_forward(low_weights):
                    def product(bank, w, k, m, high, low, first, last):
                        at, _, outs = FFN_W[w]
                        at += k * outs + m * P
                        wh, wl = W["w_hi"][:, at:at + P], W["w_lo"][:, at:at + P]
                        pe.matmul(bank, wh, high, start=first, stop=False)
                        if low_weights:
                            pe.matmul(bank, wl, high, start=False, stop=False)
                        return pe.matmul(bank, wh, low, start=False, stop=last)

                    def hidden(w, layer, j, m, ks):
                        for k in ks:
                            if m == 0 or (m == 1 and k == MT - 1):
                                pe.wait_ge(hi_ready, HIGHS * j + (layer - 1) * MT + k + 1)
                                wait_low(pe, j, layer - 1, k)
                            last = product(ring[m][:, :], w, k, m, hi[(layer - 1) % 2][:, k, :],
                                           lo[(layer - 1) % 2][:, k, :], k == 0, k == MT - 1)
                        if ks[-1] == MT - 1:
                            last.then_inc(hid_ready, 1)

                    def body(i, j, u):
                        pe.wait_ge(xh_ready, j + 1)
                        pe.wait_ge(xl_ready, j + 1)
                        for m in range(MT):
                            if m == 2:
                                project(j + 1)
                            if m >= 2:
                                pe.wait_ge(prod_done, MT * j + m - 1)
                            for n, w in enumerate(("w1", "w2")):
                                product(ring[2 * m % 4 + n][:, :], w, 0, m, xh[:, :], xl[:, :], True, True)\
                                    .then_inc(in_ready, 1)
                        for layer, w in ((1, "h1"), (2, "h2")):
                            if layer == 1:
                                pe.wait_ge(prod_done, MT * j + MT - 1)
                            hidden(w, layer, j, 0, range(MT - 1))
                            hidden(w, layer, j, 1, range(MT - 1))
                            if layer == 1:
                                o_turn(j)
                            hidden(w, layer, j, 0, [MT - 1])
                            hidden(w, layer, j, 1, [MT - 1])
                            if layer == 2:
                                n_turn(j + 1)
                            hidden(w, layer, j, 2, range(MT))
                            hidden(w, layer, j, 3, range(MT))
                        pe.wait_ge(on_ready, j + 1)
                        pe.wait_ge(xl_ready, 1 + j + 1)
                        for k in range(MT):
                            if k == MT - 1:
                                for c in range(KV):
                                    y_turn(i + 1, u, c)
                            pe.wait_ge(hi_ready, HIGHS * j + 2 * MT + k + 1)
                            wait_low(pe, j, 2, k)
                            last = product(psN[:, :], "w3", k, 0, hi[0][:, k, :], lo[0][:, k, :],
                                           k == 0, k == MT - 1)
                        last.then_inc(o_ready, 1)
                    groups(pe, body)

                for c in range(KV):
                    y_turn(0, 0, c)
                project(0)
                pe.wait_ge(cut_found, 1)
                pe.matmul(psN[0:1, 0:1], cut[:, :], W["ones"][:, :], start=True, stop=True).then_inc(cut_counted, 1)
                for c in range(KV):
                    y_turn(0, 1, c)
                pe.wait_ge(cut_known, 1)
                n_turn(0)
                any_low = pe.value_load(cut_count[0:1, 0:1], min_val=0, max_val=P)
                with pe.If(any_low == 0):
                    feed_forward(False)
                with pe.Else():
                    feed_forward(True)
                o_turn(GROUPS)


def kernel(L0_attn_x, L0_attn_wq, L0_attn_wk_down, L0_attn_wv_down, L0_attn_wk_up, L0_attn_wv_up, L0_attn_wo,
           L0_ffn_w1_w, L0_ffn_w1_s, L0_ffn_w2_w, L0_ffn_w2_s, L0_ffn_h1_w, L0_ffn_h1_s, L0_ffn_h2_w, L0_ffn_h2_s,
           L0_ffn_w3_w, L0_ffn_w3_s):
    import concourse.bacc as bacc
    from concourse.bass_utils import run_bass_kernel_spmd

    f = lambda a: np.ascontiguousarray(np.asarray(a))
    column = lambda s: f(np.asarray(s).reshape(-1, P).T)
    tiles = lambda w: np.asarray(w).T.reshape(-1, P, np.asarray(w).shape[0]).transpose(1, 0, 2).reshape(P, -1)
    ins = {
        "x": f(L0_attn_x).reshape(TOK, DM), "wqT": f(np.asarray(L0_attn_wq).T), "wkd": f(L0_attn_wk_down),
        "wvd": f(L0_attn_wv_down), "wkuT": f(np.asarray(L0_attn_wk_up).T), "wvuT": f(np.asarray(L0_attn_wv_up).T),
        "wo": f(L0_attn_wo), "ffn_w": np.concatenate([tiles(w) for w in (L0_ffn_w1_w, L0_ffn_w2_w, L0_ffn_h1_w,
                                                                  L0_ffn_h2_w, L0_ffn_w3_w)], axis=1), "s1": column(L0_ffn_w1_s), "s2": column(L0_ffn_w2_s),
        "sh1": column(L0_ffn_h1_s), "sh2": column(L0_ffn_h2_s), "s3": column(L0_ffn_w3_s),
    }
    nc = bacc.Bacc("TRN2", target_bir_lowering=False, num_devices=1)
    aps = {n: nc.dram_tensor("in_" + n, a.shape, F32, kind="ExternalInput").ap() for n, a in ins.items()}
    out = nc.dram_tensor("out_0", (TOK, DM), F32, kind="ExternalOutput").ap()
    layer(nc, *[aps[n] for n in ins], out)
    r = run_bass_kernel_spmd(nc, [{"in_" + n: a for n, a in ins.items()}], core_ids=[0])
    return r.results[0]["out_0"].reshape(BATCH, SEQ, DM)
```

```python
import numpy as np
import concourse.bass as bass
from concourse import mybir
from contextlib import ExitStack

F32 = mybir.dt.float32
F32R = mybir.dt.float32r
BF16 = mybir.dt.bfloat16
F16 = mybir.dt.float16
ALU = mybir.AluOpType
ACT = mybir.ActivationFunctionType
AX = mybir.AxisListType
ds = bass.ds

P = 128
BATCH, SEQ, DM = 2, 2048, 128
TOK = BATCH * SEQ
HEADS, KV, HD, LAT = 8, 2, 128, 32
REP = HEADS // KV
HID = 512
FFN_W, FFN_COLS = {}, 0
for _name, _in, _out in (("w1", DM, HID), ("w2", DM, HID), ("h1", HID, HID), ("h2", HID, HID), ("w3", HID, DM)):
    FFN_W[_name] = (FFN_COLS, _in // 128, _out)
    FFN_COLS += _in // 128 * _out
EPS = 1e-5
GT = 512
TPG = GT // P
GROUPS = TOK // GT
QG = SEQ // GT
KT = SEQ // P
VW = LAT + 1
VPARTS = 3
VC = VPARTS * VW
SROWS = 3 * LAT
SCALE = float(HD) ** -0.5
NEG = -1e30
PSHIFT = 14.0 * float(np.log(2.0))


STORES = KV + 3


class Chain:

    def __init__(self, eng, sem, base=0):
        self.eng, self.sem, self.base, self.n = eng, sem, base, 0

    def __call__(self, ins):
        self.n += 1
        ins.then_inc(self.sem, 1)
        self.eng.wait_ge(self.sem, self.base + self.n)


def layer(nc, x, wqT, wkd, wvd, wkuT, wvuT, wo, ffn_w, s1, s2, sh1, sh2, s3, out):
    q_dram = nc.dram_tensor("q_parts", [2, HEADS * LAT, TOK], F32, kind="Internal").ap()
    k_dram = nc.dram_tensor("k_parts", [2, KV * LAT, TOK], F32, kind="Internal").ap()
    v_dram = nc.dram_tensor("v_parts", [P, KV, TOK // P, VC], BF16, kind="Internal").ap()
    with ExitStack() as keep:
        sb = lambda name, shape, dt: keep.enter_context(nc.sbuf_tensor(name, shape, dt))
        W = {}
        W["ident"] = sb("ident", [P, P], F32)
        W["identb"] = sb("identb", [P, P], BF16)
        W["mhalf"] = sb("mhalf", [P, TPG], F32)
        W["eps"] = sb("eps", [P, TPG], F32)
        W["wo_eff"] = sb("wo_eff", [P, KV, DM], F32)
        W["w_hi"] = sb("ffn_w_hi", [P, FFN_COLS], F32R)
        W["w_lo"] = sb("ffn_w_lo", [P, FFN_COLS], F32R)
        W["w_cut"] = sb("ffn_w_cut", [P, FFN_COLS // HEADS], BF16)
        W["ones"] = sb("ones", [P, 1], F32)
        W["x"] = sb("x_all", [P, TOK // P, DM], F32)
        W["s1"], W["s2"], W["sh1"], W["sh2"] = (sb("scale_" + n, [P, 4], F32) for n in ("w1", "w2", "h1", "h2"))
        W["s3"] = sb("scale_w3", [P, 1], F32)
        W["y"] = sb("y_lat", [P, BATCH * KT, HEADS * LAT], F32)
        ql = [sb(f"ql{c}", [P, TOK], F32R) for c in range(KV)]
        F = Front(nc, keep, W, ql)
        with ExitStack() as stay:
            sa = lambda name, shape, dt: stay.enter_context(nc.sbuf_tensor(name, shape, dt))
            A = {}
            A["qs"] = [sa(f"qs{e}", [P, SEQ], F32R) for e in range(BATCH)]
            A["ks"] = [sa(f"ks{e}", [P, SEQ], F32R) for e in range(BATCH)]
            A["vs"] = [sa(f"vs{e}", [P, KT, VC], BF16) for e in range(BATCH)]
            A["mask_q"] = sa("mask_q", [P, P], BF16)
            A["mask_k"] = sa("mask_k", [P, P], BF16)
            A["shift"] = sa("shift", [P, 1], F32)
            A["mcols"] = sa("mcols", [P, TPG, P], BF16)
            A["ql"] = ql
            for name in ("qk_loaded", "v_loaded", "latents_stored"):
                A[name] = [stay.enter_context(nc.semaphore(f"{name}{n}")) for n in range(2)]
            prepare(nc, W, A, x, wqT, wkd, wvd, wkuT, wvuT, wo, ffn_w, s1, s2, sh1, sh2, s3,
                    q_dram, k_dram, v_dram)
            attend(nc, W, A, F, ffn_w, q_dram, k_dram, v_dram)
        finish(nc, W, F, out)


def load_qk(sp, A, q_dram, k_dram, h, e):
    tok = slice(e * SEQ, (e + 1) * SEQ)
    for n in range(2):
        sp.dma_start(A["qs"][e][n * LAT:(n + 1) * LAT, :].bitcast(F32),
                     q_dram[0, ds(h * LAT, LAT), tok]).then_inc(A["qk_loaded"][e], 16)
    first = isinstance(h, int) and h == 0
    low = A["ql"][0][0:LAT, tok].bitcast(F32) if first else q_dram[1, ds(h * LAT, LAT), tok]
    sp.dma_start(A["qs"][e][2 * LAT:3 * LAT, :].bitcast(F32), low).then_inc(A["qk_loaded"][e], 16)
    for n, part in enumerate((0, 1, 0)):
        sp.dma_start(A["ks"][e][n * LAT:(n + 1) * LAT, :].bitcast(F32),
                     k_dram[part, ds(h // REP * LAT, LAT), tok]).then_inc(A["qk_loaded"][e], 16)


def load_v(sp, A, v_dram, h, e):
    sp.dma_start(A["vs"][e][:, :, :], v_dram[:, ds(h // REP, 1), e * KT:(e + 1) * KT, :]
                 .rearrange("p o t c -> p (o t) c")).then_inc(A["v_loaded"][e], 16)


class Front:

    def __init__(self, nc, keep, W, ql):
        sb = lambda name, shape, dt: keep.enter_context(nc.sbuf_tensor("fr_" + name, shape, dt))
        sem = lambda name: keep.enter_context(nc.semaphore("fr_" + name))
        self.W = W
        spare = ql[0][:, :].bitcast(F32)
        at = 0
        def take(columns):
            nonlocal at
            at += columns
            return spare[:, at - columns:at]
        self.ys = [take(TPG * HEADS * LAT).rearrange("p (t l) -> p t l", t=TPG) for _ in range(2)]
        self.yT = take(KV * GT).rearrange("p (c q) -> p c q", c=KV)
        self.nrm = take(GT).rearrange("p (t d) -> p t d", t=TPG)
        self.xn = take(GT).rearrange("p (t d) -> p t d", t=TPG)
        self.xh, self.xl = (ql[1][:, n * GT:(n + 1) * GT] for n in range(2))
        self.stats = {n: sb(f"stats_{n}", [P, TPG, 6], F32) for n in "abo"}
        self.mv = {n: sb(f"mv_{n}", [P, TPG, 2], F32) for n in "abo"}
        self.ve = {n: sb(f"ve_{n}", [P, TPG], F32) for n in "abo"}
        self.rstd = {n: sb(f"rstd_{n}", [P, TPG], F32) for n in "abo"}
        self.held = {n: sb("held_" + n, [P, 1], F32) for n in "abox"}
        self.held_p = sb("held_p", [P, 1], F32)
        self.cut = sb("cut", [P, 1], F32)
        self.cut_count = sb("cut_count", [1, 1], mybir.dt.int32)
        self.y_loaded = [sem(f"y_loaded{u}") for u in range(2)]
        self.y_turned, self.yT_ready, self.a_ready = sem("y_turned"), sem("yT_ready"), sem("a_ready")
        self.stats_ready = {n: sem(f"stats_{n}") for n in "abo"}
        self.mv_ready = {n: sem(f"mv_ready_{n}") for n in "abo"}
        self.rstd_ready = {n: sem(f"rstd_{n}") for n in "abo"}
        self.ve_ready = {n: sem(f"ve_{n}") for n in "abo"}
        self.nrm_ready, self.x1_ready, self.xn_ready = sem("nrm_ready"), sem("x1_ready"), sem("xn_ready")
        self.n_turned, self.xh_ready, self.xl_ready = sem("n_turned"), sem("xh_ready"), sem("xl_ready")
        self.cut_found, self.cut_counted, self.cut_known = sem("cut_found"), sem("cut_counted"), sem("cut_known")

    def load_y(self, sp, j, u):
        sp.dma_start(self.ys[u], self.W["y"][:, ds(j % GROUPS * TPG, TPG), :]).then_inc(self.y_loaded[u], 16)

    def y_turn(self, pe, i, u, c, bank):
        pe.wait_ge(self.y_loaded[u], 16 * (i + 1))
        for t in range(TPG):
            last = pe.transpose(bank[:, t * P:(t + 1) * P], self.ys[u][:, t, c * P:(c + 1) * P],
                                self.W["ident"][:, :])
        last.then_inc(self.y_turned, 1)

    def project(self, pe, j, bank):
        pe.wait_ge(self.yT_ready, KV * (j + 1))
        for t in range(TPG):
            for c in range(KV):
                last = pe.matmul(bank[:, t * P:(t + 1) * P], self.yT[:, c, t * P:(t + 1) * P],
                                 self.W["wo_eff"][:, c, :], start=(c == 0), stop=(c == KV - 1))
        last.then_inc(self.a_ready, 1)

    def n_turn(self, pe, j, bank):
        pe.wait_ge(self.xn_ready, j + 1)
        for t in range(TPG):
            last = pe.transpose(bank[:, t * P:(t + 1) * P], self.xn[:, t, :], self.W["ident"][:, :])
        last.then_inc(self.n_turned, 1)

    def y_out(self, act, j, banks):
        for c in range(KV):
            act.wait_ge(self.y_turned, KV * j + c + 1)
            act.activation(self.yT[:, c, :], banks[c][:, :], ACT.Copy).then_inc(self.yT_ready, 1)

    def n_out(self, act, j, bank):
        act.wait_ge(self.n_turned, j + 1)
        act.activation(self.xh[:, :], bank[:, :], ACT.Copy).then_inc(self.xh_ready, 1)

    def rstd_of(self, pool, n, count):
        pool.wait_ge(self.mv_ready[n], count)
        pool.tensor_tensor(self.ve[n][:, :], self.mv[n][:, :, 1], self.W["eps"][:, :], ALU.add)\
            .then_inc(self.ve_ready[n], 1)
        pool.wait_ge(self.ve_ready[n], count)
        pool.tensor_tensor(self.rstd[n][:, :], self.ve[n][:, :], self.W["mhalf"][:, :], ALU.pow)\
            .then_inc(self.rstd_ready[n], 1)

    def carry(self, pool):
        pool.tensor_tensor(self.held_p[:, :], self.W["ones"][:, :], self.W["ones"][:, :], ALU.mult)

    def x_group(self, j):
        return self.W["x"][:, ds(j % GROUPS * TPG, TPG), :]

    def add_attention(self, pool, j):
        pool.wait_ge(self.nrm_ready, j + 1)
        self.carry(pool)
        pool.tensor_tensor(self.x_group(j), self.x_group(j), self.nrm[:, :, :], ALU.add)\
            .then_inc(self.x1_ready, 1)

    def moments(self, dve, n, count, src):
        for t in range(TPG):
            last = dve.bn_stats(self.stats[n][:, t, :], src(t))
        last.then_inc(self.stats_ready[n], 1)
        dve.wait_ge(self.stats_ready[n], count)
        dve.memset(self.held[n][:, :], 0.0)
        for t in range(TPG):
            last = dve.bn_aggr(self.mv[n][:, t, :], self.stats[n][:, t, :])
        last.then_inc(self.mv_ready[n], 1)

    def normalise(self, dve, n, count, dst, src, done):
        dve.wait_ge(self.mv_ready[n], count)
        dve.wait_ge(self.rstd_ready[n], count)
        for t in range(TPG):
            last = dve.tensor_scalar(dst[:, t, :], src(t), self.mv[n][:, t, 0:1],
                                     self.rstd[n][:, t:t + 1], ALU.subtract, ALU.mult)
        last.then_inc(done, 1)

    def attention_moments(self, dve, j, bank):
        dve.wait_ge(self.a_ready, j + 1)
        self.moments(dve, "a", j + 1, lambda t: bank[:, t * P:(t + 1) * P])

    def attention_normalise(self, dve, j, bank):
        self.normalise(dve, "a", j + 1, self.nrm, lambda t: bank[:, t * P:(t + 1) * P], self.nrm_ready)

    def x1_tile(self, j):
        return lambda t: self.W["x"][:, ds(j % GROUPS * TPG + t, 1), :].rearrange("p o d -> p (o d)")

    def x1_moments(self, dve, j):
        dve.wait_ge(self.x1_ready, j + 1)
        dve.memset(self.held["x"][:, :], 0.0)
        self.moments(dve, "b", j + 1, self.x1_tile(j))

    def x1_normalise(self, dve, j):
        self.normalise(dve, "b", j + 1, self.xn, self.x1_tile(j), self.xn_ready)

    def n_low(self, dve, j, bank):
        dve.wait_ge(self.xh_ready, j + 1)
        dve.tensor_tensor(self.xl[:, :], bank[:, :], self.xh[:, :].bitcast(F32), ALU.subtract)\
           .then_inc(self.xl_ready, 1)


def prepare(nc, W, A, x, wqT, wkd, wvd, wkuT, wvuT, wo, ffn_w, s1, s2, sh1, sh2, s3,
            q_dram, k_dram, v_dram):
    with ExitStack() as ctx:
        sb = lambda name, shape, dt: ctx.enter_context(nc.sbuf_tensor(name, shape, dt))
        sem = lambda name: ctx.enter_context(nc.semaphore(name))
        psum = lambda name, shape: ctx.enter_context(nc.psum_tensor(name, shape, F32))
        half = HEADS * DM // (HEADS * LAT)
        wq_sb, wo_sb = (W["y"][:, n * half:(n + 1) * half, :].rearrange("p a (b m) -> p (a b) m", m=DM)
                        for n in range(2))
        wku = sb("wku", [P, LAT], F32)
        wvu_pad = sb("wvu_pad", [P, REP, REP, LAT], F32)
        wkd_sb = sb("wkd_sb", [P, KV * LAT], F32)
        wvd_sb = sb("wvd_sb", [P, KV * LAT], F32)
        q_w = sb("q_w", [P, KV, P], F32)
        bst = [sb(f"bst{u}", [P, TPG, 6], F32) for u in range(2)]
        mv = [sb(f"mv{u}", [P, TPG, 2], F32) for u in range(2)]
        ve = [sb(f"ve{u}", [P, TPG], F32) for u in range(2)]
        rstd = [sb(f"rstd{u}", [P, TPG], F32) for u in range(2)]
        rows = GT // (HEADS * LAT)
        spare = [W["y"][:, 2 * half + n * rows:2 * half + (n + 1) * rows, :] for n in range(4)]
        xn = [a.rearrange("p a (b d) -> p (a b) d", d=DM) for a in spare[:2]]
        xnT = [a.rearrange("p a b -> p (a b)") for a in spare[2:]]
        qh = [sb(f"qh{u}", [P, KV, GT], F32R) for u in range(2)]
        kh = [sb(f"kh{u}", [KV * LAT, GT], F32R) for u in range(2)]
        kl = [sb(f"kl{u}", [KV * LAT, GT], F32R) for u in range(2)]
        vp = [sb(f"vp{u}", [P, KV, TPG, VC], BF16) for u in range(2)]
        vf = [sb(f"vf{u}", [P, KV, TPG, LAT], F32) for u in range(2)]
        zeros = sb("zeros", [P, KV, TPG, LAT], F32)
        held = sb("held", [P, 1], F32)
        psT = [psum(f"psT{u}", [P, GT]) for u in range(2)]
        psK = psum("psK", [P, GT])
        psQ = [psum(f"psQ{c}", [P, GT]) for c in range(KV)]
        psV = psum("psV", [P, TPG, KV * LAT])
        psA = psum("psA", [P, KV, P])
        psW = psum("psW", [P, KV, P])

        w_loaded = sem("w_loaded")
        ffn_loaded = sem("ffn_loaded")
        consts = sem("consts")
        x_loaded = [sem(f"x_loaded{n}") for n in range(2)]
        mv_ready = sem("mv_ready")
        rstd_ready = sem("rstd_ready")
        xn_ready = sem("xn_ready")
        t_ready = sem("t_ready")
        xnT_ready = sem("xnT_ready")
        proj_ready = sem("proj_ready")
        w_ready = sem("w_ready")
        qw_ready = sem("qw_ready")
        hi_ready = sem("hi_ready")
        lo_ready = sem("lo_ready")
        v_ready = sem("v_ready")
        vf_ready = sem("vf_ready")
        stored = A["latents_stored"]
        d1 = sem("dve_chain")
        d2 = sem("dve_ones")
        p1 = sem("pool_chain")
        v_chain = sem("v_chain")
        mask_chain = sem("mask_chain")

        X_CUTS = (0, 2 * TPG, TOK // P)

        def load_x(sp, n):
            a, b = X_CUTS[n], X_CUTS[n + 1]
            sp.dma_start(W["x"][:, a:b, :], x[a * P:b * P, :].rearrange("(t p) d -> p t d", p=P))\
              .then_inc(x_loaded[n], 16)

        with nc.Block() as block:

            @block.sync
            def _(sp):
                load_x(sp, 0)
                sp.dma_start(wq_sb[:, :, :], wqT.rearrange("(h d) m -> d h m", d=HD)).then_inc(w_loaded, 16)
                sp.dma_start(wku[:, :], wkuT).then_inc(w_loaded, 16)
                sp.dma_start(wkd_sb[:, :], wkd).then_inc(w_loaded, 16)
                sp.dma_start(wvd_sb[:, :], wvd).then_inc(w_loaded, 16)
                sp.dma_start(wo_sb[:, :, :], wo.rearrange("(h d) m -> d h m", d=HD)).then_inc(w_loaded, 16)
                sp.wait_ge(consts, 1)
                for r in range(REP):
                    sp.dma_start(wvu_pad[:, r, r, :], wvuT).then_inc(w_loaded, 16)
                load_x(sp, 1)
                for n, s in (("s1", s1), ("s2", s2), ("sh1", sh1), ("sh2", sh2), ("s3", s3)):
                    sp.dma_start(W[n][:, :], s).then_inc(ffn_loaded, 16)
                for e in range(BATCH):
                    with sp.Fori(e * QG // 2, (e + 1) * QG // 2) as i:
                        for u in range(2):
                            tok = ds(sp.snap((2 * i + u) * GT), GT)
                            tiles = ds(sp.snap((2 * i + u) * TPG), TPG)
                            sp.wait_ge(lo_ready, 3 * (2 * i + u + 2))
                            for c in range(KV):
                                sp.dma_start(q_dram[0, c * P:(c + 1) * P, tok], qh[u][:, c, :].bitcast(F32))\
                                  .then_inc(stored[u], 16)
                            sp.dma_start(k_dram[0, :, tok], kh[u][:, :].bitcast(F32)).then_inc(stored[u], 16)
                            sp.dma_start(k_dram[1, :, tok], kl[u][:, :].bitcast(F32)).then_inc(stored[u], 16)
                            sp.wait_ge(v_ready, 2 * i + u + 1)
                            sp.dma_start(v_dram[:, :, tiles, :], vp[u][:, :, :, :]).then_inc(stored[u], 16)
                    if e == 0:
                        for u in range(2):
                            sp.wait_ge(stored[u], STORES * 16 * (QG // 2 + 1))
                        sp.wait_ge(lo_ready, 3 * (QG + 1))
                        load_qk(sp, A, q_dram, k_dram, 0, 0)
                        load_v(sp, A, v_dram, 0, 0)
                sp.wait_ge(ffn_loaded, 16 * 5)

            @block.gpsimd
            def _(pool):
                pool.memset(wvu_pad[:, :, :, :], 0.0).then_inc(consts, 1)
                pool.memset(W["mhalf"][:, :], -0.5)
                pool.memset(W["eps"][:, :], EPS)
                pool.memset(W["ones"][:, :], 1.0)
                pool.memset(W["w_cut"][:, :], 0.0)
                pool.memset(zeros[:, :, :, :], 0.0)
                pool.memset(W["ident"][:, :], 0.0).then_inc(p1, 1)
                pool.wait_ge(p1, 1)
                pool.affine_select(out=W["ident"][:, :], in_=W["ident"][:, :], compare_op=ALU.not_equal, fill=1.0,
                                   base=0, pattern=[[-1, P]], channel_multiplier=1).then_inc(p1, 1)
                pool.wait_ge(p1, 2)
                pool.tensor_copy(W["identb"][:, :], W["ident"][:, :]).then_inc(consts, 1)

                link = Chain(pool, mask_chain)
                link(pool.memset(A["mask_q"][:, :], 0.0))
                link(pool.affine_select(out=A["mask_q"][:, :], in_=A["mask_q"][:, :], compare_op=ALU.is_ge, fill=NEG,
                                        base=0, pattern=[[-1, P]], channel_multiplier=1))
                link(pool.memset(A["mask_k"][:, :], 0.0))
                link(pool.affine_select(out=A["mask_k"][:, :], in_=A["mask_k"][:, :], compare_op=ALU.is_ge, fill=NEG,
                                        base=0, pattern=[[1, P]], channel_multiplier=-1))

                def rstd_of(j, u):
                    pool.wait_ge(mv_ready, j + 1)
                    pool.tensor_tensor(ve[u][:, :], mv[u][:, :, 1], W["eps"][:, :], ALU.add).then_inc(p1, 1)
                    pool.wait_ge(p1, 2 + j + 1)
                    pool.tensor_tensor(rstd[u][:, :], ve[u][:, :], W["mhalf"][:, :], ALU.pow).then_inc(rstd_ready, 1)

                rstd_of(0, 0)
                rstd_of(1, 1)
                with pool.Fori(0, GROUPS // 2) as i:
                    for u in range(2):
                        j = 2 * i + u
                        rstd_of(j + 2, u)
                        pool.wait_ge(vf_ready, 1 + j + 1)
                        v = vf[u][:, :, :, :]
                        part = [vp[u][:, :, :, VW * n:VW * n + LAT] for n in range(VPARTS)]
                        link = Chain(pool, v_chain, 2 * j)
                        link(pool.tensor_tensor(v, v, part[0], ALU.subtract))
                        link(pool.tensor_tensor(part[1], v, zeros[:, :, :, :], ALU.add))
                        pool.tensor_tensor(part[2], v, part[1], ALU.subtract).then_inc(v_ready, 1)

            @block.scalar
            def _(act):
                act.sem_inc(vf_ready, 1)
                act.wait_ge(qw_ready, 1)
                act.activation(q_w[:, :, :], psA[:, :, :], ACT.Copy).then_inc(w_ready, 1)
                act.wait_ge(qw_ready, 2)
                act.activation(W["wo_eff"][:, :, :], psW[:, :, :], ACT.Copy).then_inc(w_ready, 1)

                def xnT_out(j, u):
                    act.wait_ge(t_ready, j + 1)
                    act.activation(xnT[u][:, :], psT[u][:, :], ACT.Copy).then_inc(xnT_ready, 1)

                xnT_out(0, 0)
                with act.Fori(0, GROUPS // 2) as i:
                    for u in range(2):
                        j = 2 * i + u
                        act.wait_ge(stored[u], STORES * 16 * (i + 1))
                        act.wait_ge(proj_ready, 4 * j + 1)
                        act.activation(kh[u][:, :], psK[0:KV * LAT, :], ACT.Copy).then_inc(hi_ready, 1)
                        xnT_out(j + 1, 1 - u)
                        for c in range(KV):
                            act.wait_ge(proj_ready, 4 * j + 2 + c)
                            act.activation(qh[u][:, c, :], psQ[c][:, :], ACT.Copy).then_inc(hi_ready, 1)
                        act.wait_ge(proj_ready, 4 * j + 4)
                        v = psV[:, :, :].rearrange("p t (c l) -> p c t l", c=KV)
                        act.activation(vf[u][:, :, :, :], v, ACT.Copy)
                        act.activation(vp[u][:, :, :, 0:LAT], v, ACT.Copy).then_inc(vf_ready, 1)

            @block.vector
            def _(dve):
                for u in range(2):
                    dve.memset(vp[u][:, :, :, :], 0.0).then_inc(d1, 1)
                dve.wait_ge(d1, 2)
                for u in range(2):
                    dve.memset(vp[u][:, :, :, LAT:LAT + 1], 1.0).then_inc(d1, 1)
                dve.wait_ge(d1, 4)
                for u in range(2):
                    dve.sem_inc(stored[u], STORES * 16)
                dve.sem_inc(lo_ready, 3)

                def x_tile(j, t):
                    return W["x"][:, ds(j % GROUPS * TPG + t, 1), :].rearrange("p o d -> p (o d)")

                def moments(j, u):
                    for t in range(TPG):
                        last = dve.bn_stats(bst[u][:, t, :], x_tile(j, t))
                    last.then_inc(d1, 1)
                    dve.wait_ge(d1, 4 + j + 1)
                    dve.memset(held[:, :], 0.0)
                    for t in range(TPG):
                        last = dve.bn_aggr(mv[u][:, t, :], bst[u][:, t, :])
                    last.then_inc(mv_ready, 1)

                def normalise(j, u):
                    dve.wait_ge(mv_ready, j + 1)
                    dve.wait_ge(rstd_ready, j + 1)
                    for t in range(TPG):
                        last = dve.tensor_scalar(xn[u][:, t, :], x_tile(j, t), mv[u][:, t, 0:1],
                                                 rstd[u][:, t:t + 1], ALU.subtract, ALU.mult)
                    last.then_inc(xn_ready, 1)

                for e in range(BATCH):
                    dve.memset(A["ks"][e][SROWS:P, :].bitcast(F32), 0.0).then_inc(d2, 1)
                dve.memset(A["mcols"][:, :, :], 0.0)
                dve.memset(A["shift"][:, :], PSHIFT)
                dve.wait_ge(d2, BATCH)
                for e in range(BATCH):
                    dve.memset(A["ks"][e][SROWS:SROWS + 2, :].bitcast(F32), 1.0)
                dve.wait_ge(x_loaded[0], 16)
                for j in range(2):
                    moments(j, j)
                for j in range(2):
                    normalise(j, j)
                dve.wait_ge(x_loaded[1], 16)
                with dve.Fori(0, GROUPS // 2) as i:
                    for u in range(2):
                        j = 2 * i + u
                        moments(j + 2, u)
                        dve.wait_ge(hi_ready, 3 * j + 1)
                        dve.tensor_tensor(kl[u][:, :], psK[0:KV * LAT, :], kh[u][:, :].bitcast(F32), ALU.subtract)\
                           .then_inc(lo_ready, 1)
                        for c in range(KV):
                            dve.wait_ge(hi_ready, 3 * j + 2 + c)
                            dve.tensor_tensor(A["ql"][c][:, ds(j * GT, GT)], psQ[c][:, :], qh[u][:, c, :].bitcast(F32),
                                              ALU.subtract).then_inc(lo_ready, 1)
                            if c == 0:
                                dve.wait_ge(t_ready, j + 1)
                                normalise(j + 2, u)

            @block.tensor
            def _(pe):
                pe.wait_ge(w_loaded, 16 * 9)
                for h in range(HEADS):
                    c, r = divmod(h, REP)
                    last = pe.matmul(psA[:, c, r * LAT:(r + 1) * LAT], wq_sb[:, h, :], wku[:, :],
                                     start=True, stop=True)
                last.then_inc(qw_ready, 1)
                for c in range(KV):
                    for r in range(REP):
                        last = pe.matmul(psW[:, c, :], wvu_pad[:, r, :, :].rearrange("p a l -> p (a l)"),
                                         wo_sb[:, c * REP + r, :], start=(r == 0), stop=(r == REP - 1))
                last.then_inc(qw_ready, 1)
                pe.wait_ge(consts, 2)
                pe.wait_ge(w_ready, 1)

                def turn(j, u):
                    pe.wait_ge(xn_ready, j + 1)
                    for t in range(TPG):
                        last = pe.transpose(psT[u][:, t * P:(t + 1) * P], xn[u][:, t, :], W["ident"][:, :])
                    last.then_inc(t_ready, 1)

                turn(0, 0)
                with pe.Fori(0, GROUPS // 2) as i:
                    for u in range(2):
                        j = 2 * i + u
                        pe.wait_ge(xnT_ready, j + 1)
                        pe.wait_ge(lo_ready, 3 * j + 1)
                        pe.matmul(psK[0:KV * LAT, :], wkd_sb[:, :], xnT[u][:, :], start=True, stop=True)\
                          .then_inc(proj_ready, 1)
                        turn(j + 1, 1 - u)
                        for c in range(KV):
                            pe.wait_ge(lo_ready, 3 * j + 2 + c)
                            pe.matmul(psQ[c][:, :], q_w[:, c, :], xnT[u][:, :], start=True, stop=True)\
                              .then_inc(proj_ready, 1)
                        pe.wait_ge(vf_ready, j + 1)
                        for t in range(TPG):
                            last = pe.matmul(psV[:, t, :], xnT[u][:, t * P:(t + 1) * P], wvd_sb[:, :],
                                             start=True, stop=True)
                        last.then_inc(proj_ready, 1)


LAG = 3
NP_BUF = 5
JOBS = BATCH * QG
LEAD = 28
TURN = 2
POOL_SHARE = 0.84
POOL_SHARE_END = 0.4


NEXT = {name: STEP for STEP, names in {
    27: ("y_turn",), 28: ("y_out", "project"), 29: ("attention_moments", "attention_rstd"),
    30: ("attention_normalise", "add_attention"), 31: (), 32: ("x1_moments", "x1_rstd"),
    33: (), 34: ("x1_normalise",), 35: ("n_turn", "n_out"), 36: ("n_low", "cut"), 37: ("y_turn_1", "y_out_1"),
}.items() for name in names}


class Pair:

    def __init__(self, job, first):
        self.job, self.e, self.g = job, job // QG, job % QG
        self.tiles, at = [], 0
        for kt in (first, first + 1):
            q0 = max(0, kt - TPG * self.g) * P
            self.tiles.append((kt, q0, at, kt >= TPG * self.g))
            at += GT - q0
        self.width = at
        self.first = first == 0
        self.last = first + 2 == TPG * (self.g + 1)


PAIRS = [Pair(job, first) for job in range(JOBS) for first in range(0, TPG * (job % QG + 1), 2)]
STEPS = len(PAIRS)
TAIL = STEPS
CHUNKS = [(job, t, c, GT if c < job % QG else (t + 1) * P)
          for job in range(JOBS) for t in range(TPG) for c in range(job % QG + 1)]
NCH = len(CHUNKS)
SHARE = [[LEAD + n for n in range(NCH) if min(n // 2, STEPS) == p or (p == TAIL and n // 2 == STEPS - 1)]
         for p in range(STEPS + 1)]
SHARE[STEPS - 1] = []


def ends_job(n):
    return n % NCH == NCH - 1 or CHUNKS[(n + 1) % NCH][0] != CHUNKS[n % NCH][0]


TURNS = [[(n // NCH, CHUNKS[n % NCH][0]) for p in range(STEPS + 1) for n in SHARE[p]
          if ends_job(n) and min(p + TURN, TAIL) == step] for step in range(STEPS + 1)]
PRE_TURNS = [CHUNKS[n][0] for n in range(LEAD) if ends_job(n)]
for _step, _turns in enumerate(TURNS):
    for _ahead, _job in _turns:
        assert _step < _ahead * STEPS + min(p for p in range(STEPS) if PAIRS[p].job == _job) - LAG


def rest_columns(k, last=False):
    width = PAIRS[k % STEPS].width
    cut = int(width * (POOL_SHARE_END if last and k > (NCH - LEAD) // 2 + LAG else POOL_SHARE)) // 64 * 64
    return slice(0, cut), slice(cut, width)


def ended(p):
    return PAIRS[p].job if 0 <= p < STEPS and PAIRS[p].last else None


def attend(nc, W, A, F, ffn_w, q_dram, k_dram, v_dram):
    with ExitStack() as ctx:
        sb = lambda name, shape, dt: ctx.enter_context(nc.sbuf_tensor(name, shape, dt))
        sem = lambda name: ctx.enter_context(nc.semaphore("a_" + name))
        psum = lambda name, shape: ctx.enter_context(nc.psum_tensor(name, shape, F32))
        qs, ks, vs, mask_q, mask_k, shift, mcols = (A[n] for n in ("qs", "ks", "vs", "mask_q", "mask_k", "shift",
                                                                   "mcols"))
        qk_loaded, v_loaded = A["qk_loaded"], A["v_loaded"]
        mpart = [sb(f"mpart{n}", [P, TPG, QG], F32) for n in range(2)]
        nmax = sb("nmax", [P, TPG], F32)
        sums = sb("sums", [P, TPG, VW], F32)
        rden = sb("rden", [P, TPG], F32)
        w_raw = sb("ffn_w_raw", [P, FFN_COLS // HEADS], F32)
        acc_sb = [sb(f"acc_sb{n}", [VC, GT], F32) for n in range(2)]
        prob = [sb(f"prob{n}", [P, 2 * GT], F32) for n in range(NP_BUF)]
        rest = [sb(f"rest{n}", [P, 2 * GT], F16) for n in range(NP_BUF)]
        s_max = [psum(f"s_max{n}", [P, GT]) for n in range(2)]
        s_t = [psum(f"s_t{n}", [P, 2 * GT]) for n in range(2)]
        acc = [psum(f"acc{n}", [P, GT]) for n in range(2)]
        turned_sums = [acc[n][:, :].rearrange("p (t q) -> p t q", q=P) for n in range(2)]
        turned_max = [acc[n][:, :].bitcast(BF16)[:, 0:GT] for n in range(2)]

        w_loaded, lows_stored = sem("w_loaded"), sem("lows_stored")
        w_hi_ready, w_lo_ready, cut_noted = sem("w_hi_ready"), sem("w_lo_ready"), sem("cut_noted")
        smax_ready = sem("smax_ready")
        max_done = sem("max_done")
        nmax_chain = sem("nmax_chain")
        nmax_ready = sem("nmax_ready")
        turn_ready = sem("turn_ready")
        mrow_ready = sem("mrow_ready")
        st_ready = sem("st_ready")
        exp_done = sem("exp_done")
        rest_pool = sem("rest_pool")
        rest_dve = sem("rest_dve")
        pv_done = sem("pv_done")
        acc_copied = sem("acc_copied")
        sums_ready = sem("sums_ready")
        y_chain = sem("y_chain")
        y_read = sem("y_read")
        y_done = sem("y_done")
        FREE_MAX, FREE_ST, FREE_P, FREE_Y, FREE_SUMS = 2, 2, NP_BUF, 2, 1

        def turns(p, h, last):
            return [(job, (h + ahead) * JOBS + job) for ahead, job in TURNS[p] if not (ahead and last)]

        def share(p, last):
            return [n for n in SHARE[p] if not (last and n >= NCH)]

        def other_bank(p):
            return 1 - PAIRS[p].job % 2

        def pair_at(k, last):
            return None if last and k >= STEPS else k

        def heads(body):
            def run(eng):
                with eng.Fori(0, HEADS - 1) as h:
                    body(h, False)
                body(HEADS - 1, True)
            return run

        def take_rest(eng, k, number, columns, done):
            n = k % NP_BUF
            eng.wait_ge(exp_done, FREE_ST + number + 1)
            eng.tensor_tensor(rest[n][:, columns], prob[n][:, columns],
                              prob[n][:, :].bitcast(BF16)[:, 1::2][:, columns], ALU.subtract).then_inc(done, 1)

        with nc.Block() as block:

            @block.sync
            def _(sp):
                def load_w(h):
                    sp.dma_start(w_raw[:, :], ffn_w[:, ds(h * (FFN_COLS // HEADS), FFN_COLS // HEADS)])\
                      .then_inc(w_loaded, 16)

                for u in range(2):
                    sp.wait_ge(A["latents_stored"][u], STORES * 16 * (GROUPS // 2 + 1))
                load_qk(sp, A, q_dram, k_dram, 0, 1)
                load_v(sp, A, v_dram, 0, 1)
                load_w(0)
                for c in range(KV):
                    sp.dma_start(q_dram[1, c * P:(c + 1) * P, :], A["ql"][c][:, :].bitcast(F32))\
                      .then_inc(lows_stored, 16)
                sp.wait_ge(lows_stored, KV * 16)
                with sp.Fori(0, HEADS - 1) as h:
                    sp.wait_ge(w_lo_ready, h + 1)
                    load_w(h + 1)
                    for e in range(BATCH):
                        sp.wait_ge(st_ready, h * STEPS + STEPS // BATCH * (e + 1))
                        load_qk(sp, A, q_dram, k_dram, h + 1, e)
                        sp.wait_ge(pv_done, FREE_P + h * STEPS + STEPS // BATCH * (e + 1))
                        load_v(sp, A, v_dram, h + 1, e)
                for j in range(2):
                    sp.wait_ge(y_chain, FREE_SUMS + 2 * ((HEADS - 1) * JOBS + j + 1))
                    F.load_y(sp, j, j)

            @block.gpsimd
            def _(pool):
                for k in range(LAG):
                    take_rest(pool, k, k, rest_columns(k)[0], rest_pool)

                def body(h, last):
                    for p in range(STEPS):
                        k = pair_at(p + LAG, last)
                        if k is not None:
                            take_rest(pool, k, h * STEPS + k, rest_columns(k, last)[0], rest_pool)
                        if p == 2:
                            pool.wait_ge(w_hi_ready, h + 1)
                            part = ds(h * (FFN_COLS // HEADS), FFN_COLS // HEADS)
                            pool.tensor_tensor(W["w_lo"][:, part], w_raw[:, :],
                                               W["w_hi"][:, part].bitcast(F32), ALU.subtract)\
                                .then_inc(w_lo_ready, 1)
                        if last and p == NEXT["attention_rstd"]:
                            F.rstd_of(pool, "a", 1)
                        if last and p == NEXT["add_attention"]:
                            F.add_attention(pool, 0)
                        if last and p == NEXT["x1_rstd"]:
                            F.rstd_of(pool, "b", 1)
                heads(body)(pool)

            @block.scalar
            def _(act):
                act.sem_inc(exp_done, FREE_ST)

                def mrow(job, number, bank):
                    e, g = divmod(job, QG)
                    act.wait_ge(turn_ready, number + 1)
                    act.activation(qs[e][SROWS:P, g * GT:(g + 1) * GT], turned_max[bank][SROWS:P, :],
                                   ACT.Copy)\
                       .then_inc(mrow_ready, 1)

                def acc_out(p, h):
                    n = ended(p) % 2
                    act.wait_ge(pv_done, FREE_P + h * STEPS + p + 1)
                    act.activation(acc_sb[n][:, :], acc[n][0:VC, :], ACT.Copy).then_inc(acc_copied, 1)

                def exponentials(k, number):
                    width = PAIRS[k % STEPS].width
                    act.wait_ge(st_ready, number + 1)
                    act.wait_ge(pv_done, number + 1)
                    act.activation(prob[k % NP_BUF][:, 0:width], s_t[k % 2][:, 0:width], ACT.Exp,
                                   bias=shift[:, 0:1], scale=SCALE).then_inc(exp_done, 1)

                def body(h, last):
                    for p in range(STEPS + 1):
                        if p == STEPS - 1:
                            acc_out(p, h)
                        if p < STEPS and (k := pair_at(p + LAG, last)) is not None:
                            exponentials(k, h * STEPS + k)
                        for job, number in turns(p, h, last):
                            mrow(job, number, other_bank(p))
                        if p < STEPS - 1 and ended(p) is not None:
                            acc_out(p, h)
                        if last and p == NEXT["y_out"]:
                            F.y_out(act, 0, s_max)
                        if last and p == NEXT["n_out"]:
                            F.n_out(act, 0, s_max[1])
                        if last and p == NEXT["y_out_1"]:
                            F.y_out(act, 1, s_max)
                        if p == 0:
                            part = ds(h * (FFN_COLS // HEADS), FFN_COLS // HEADS)
                            act.wait_ge(w_loaded, 16 * (h + 1))
                            act.activation(W["w_hi"][:, part], w_raw[:, :], ACT.Copy)\
                               .then_inc(w_hi_ready, 1)

                for job in PRE_TURNS:
                    mrow(job, job, 1)
                for u in range(2):
                    act.wait_ge(A["latents_stored"][u], STORES * 16 * (GROUPS // 2 + 1))
                for k in range(LAG):
                    exponentials(k, k)
                heads(body)(act)

            @block.vector
            def _(dve):
                dve.sem_inc(max_done, FREE_MAX)
                dve.sem_inc(y_read, FREE_Y)
                dve.sem_inc(y_chain, FREE_SUMS)

                def maximum(n, h):
                    job, t, c, width = CHUNKS[n % NCH]
                    dve.wait_ge(smax_ready, h * NCH + n + 1)
                    dve.reduce_max(mpart[job % 2][:, t, c:c + 1], s_max[n % 2][:, 0:width], AX.X)\
                       .then_inc(max_done, 1)

                def nmax_reduce(n, h):
                    job = CHUNKS[n % NCH][0]
                    dve.wait_ge(max_done, FREE_MAX + h * NCH + n + 1)
                    dve.tensor_reduce(nmax[:, :], mpart[job % 2][:, :, 0:job % QG + 1], AX.X, ALU.max,
                                      negate=True).then_inc(nmax_chain, 1)

                def nmax_high(n, h):
                    jn = (h + n // NCH) * JOBS + CHUNKS[n % NCH][0]
                    if not (isinstance(jn, int) and jn == 0):
                        dve.wait_ge(turn_ready, jn)
                    dve.wait_ge(nmax_chain, 2 * jn + 1)
                    dve.tensor_copy(mcols[:, :, SROWS], nmax[:, :]).then_inc(nmax_chain, 1)

                def nmax_low(n, h):
                    jn = (h + n // NCH) * JOBS + CHUNKS[n % NCH][0]
                    dve.wait_ge(nmax_chain, 2 * jn + 2)
                    dve.tensor_tensor(mcols[:, :, SROWS + 1], nmax[:, :], mcols[:, :, SROWS], ALU.subtract)\
                       .then_inc(nmax_ready, 1)

                def weigh_sum(job, h):
                    dve.wait_ge(y_chain, FREE_SUMS + 2 * (h * JOBS + job))
                    dve.wait_ge(sums_ready, h * JOBS + job + 1)
                    dve.tensor_reduce(sums[:, :, :], turned_sums[job % 2][:, :, 0:VC].rearrange("p t (n c) -> p t c n", n=VPARTS),
                                      AX.X, ALU.add).then_inc(y_read, 1)

                def weigh_denominator(job, h):
                    dve.wait_ge(y_read, FREE_Y + h * JOBS + job + 1)
                    dve.reciprocal(rden[:, :], sums[:, :, LAT]).then_inc(y_chain, 1)

                def weigh_divide(job, h):
                    e, g = divmod(job, QG)
                    dve.wait_ge(y_chain, FREE_SUMS + 2 * (h * JOBS + job) + 1)
                    dve.tensor_tensor(W["y"][:, e * KT + g * TPG:e * KT + (g + 1) * TPG, ds(h * LAT, LAT)],
                                      sums[:, :, 0:LAT], rden[:, :].unsqueeze(2).to_broadcast([P, TPG, LAT]),
                                      ALU.mult).then_inc(y_chain, 1)

                def last_chunks(p, last):
                    return [n for n in share(p, last) if ends_job(n)] if p >= 0 else []

                def body(h, last):
                    for p in range(STEPS + 1):
                        chunks, maxed = share(p, last), last_chunks(p - 1, last)
                        for n in chunks[:1]:
                            maximum(n, h)
                        for n in maxed:
                            nmax_high(n, h)
                        if (job := ended(p - 3)) is not None:
                            weigh_divide(job, h)
                        if p < TAIL and (job := ended(p - 2)) is not None:
                            weigh_sum(job, h)
                        for n in chunks[1:]:
                            maximum(n, h)
                        for n in maxed:
                            nmax_low(n, h)
                        if p < STEPS:
                            k = pair_at(p + LAG - 1, last)
                            if k is not None:
                                take_rest(dve, k, h * STEPS + k, rest_columns(k, last)[1], rest_dve)
                        if p < TAIL and (job := ended(p - 2)) is not None:
                            weigh_denominator(job, h)
                        for n in last_chunks(p, last):
                            nmax_reduce(n, h)
                            if p == TAIL:
                                nmax_high(n, h)
                                nmax_low(n, h)
                        if p == TAIL:
                            job = ended(p - 1)
                            weigh_sum(job, h)
                            weigh_denominator(job, h)
                            weigh_divide(job, h)
                        if last and p == NEXT["attention_moments"]:
                            F.attention_moments(dve, 0, s_max[0])
                        if last and p == NEXT["attention_normalise"]:
                            F.attention_normalise(dve, 0, s_max[0])
                        if last and p == NEXT["x1_moments"]:
                            F.x1_moments(dve, 0)
                        if last and p == NEXT["x1_normalise"]:
                            F.x1_normalise(dve, 0)
                        if last and p == NEXT["n_low"]:
                            F.n_low(dve, 0, s_max[1])
                        if last and p == NEXT["cut"]:
                            dve.wait_ge(cut_noted, HEADS)
                            dve.reduce_max(F.cut[:, :], W["w_cut"][:, :], AX.X).then_inc(F.cut_found, 1)
                            dve.wait_ge(F.cut_counted, 1)
                            dve.tensor_copy(F.cut_count[0:1, 0:1], s_max[0][0:1, 0:1]).then_inc(F.cut_known, 1)
                        if p == STEPS // 2:
                            dve.wait_ge(w_lo_ready, h + 1)
                            part = ds(h * (FFN_COLS // HEADS), FFN_COLS // HEADS)
                            dve.scalar_tensor_tensor(out=W["w_cut"][:, :], in0=W["w_lo"][:, part].bitcast(F32),
                                                     scalar=0.0, in1=W["w_cut"][:, :], op0=ALU.not_equal,
                                                     op1=ALU.max).then_inc(cut_noted, 1)

                for n in range(LEAD):
                    maximum(n, 0)
                    if ends_job(n):
                        nmax_reduce(n, 0)
                        nmax_high(n, 0)
                        nmax_low(n, 0)
                for k in range(LAG - 1):
                    take_rest(dve, k, k, rest_columns(k)[1], rest_dve)
                heads(body)(dve)

            @block.tensor
            def _(pe):
                pe.sem_inc(pv_done, FREE_P)

                def scores_q(n, h):
                    job, t, c, width = CHUNKS[n % NCH]
                    e, g = divmod(job, QG)
                    number = h * NCH + n
                    if n % NCH in (0, NCH // BATCH):
                        pe.wait_ge(qk_loaded[e], 6 * 16 * (h + n // NCH + 1))
                    pe.wait_ge(max_done, number + 1)
                    bank = s_max[n % 2]
                    diagonal = c == g
                    q = (g * TPG + t) * P
                    last = pe.matmul(bank[:, 0:width], qs[e][0:SROWS, q:q + P],
                                     ks[e][0:SROWS, c * GT:c * GT + width], start=True, stop=not diagonal)
                    if diagonal:
                        last = pe.matmul(bank[:, width - P:width], W["identb"][:, :], mask_q[:, :],
                                         start=False, stop=True)
                    last.then_inc(smax_ready, 1)

                def scores_k(k, number, h):
                    pair = PAIRS[k % STEPS]
                    if pair.first:
                        pe.wait_ge(mrow_ready, (h + k // STEPS) * JOBS + pair.job + 1)
                    pe.wait_ge(exp_done, number + 1)
                    for kt, q0, at, diagonal in pair.tiles:
                        width = GT - q0
                        last = pe.matmul(s_t[k % 2][:, at:at + width], ks[pair.e][:, kt * P:(kt + 1) * P],
                                         qs[pair.e][:, pair.g * GT + q0:(pair.g + 1) * GT],
                                         start=True, stop=not diagonal)
                        if diagonal:
                            last = pe.matmul(s_t[k % 2][:, at:at + P], W["identb"][:, :], mask_k[:, :],
                                             start=False, stop=True)
                    last.then_inc(st_ready, 1)

                def turn_maxima(number, jobs, bank):
                    pe.wait_ge(nmax_ready, number + 1)
                    pe.wait_ge(y_read, FREE_Y + jobs)
                    if not (isinstance(number, int) and number == 0):
                        pe.wait_ge(mrow_ready, number)
                    for t in range(TPG):
                        last = pe.transpose(turned_max[bank][:, t * P:(t + 1) * P], mcols[:, t, :], W["identb"][:, :])
                    last.then_inc(turn_ready, 1)

                def turn_sums(job, number):
                    pe.wait_ge(acc_copied, number + 1)
                    for t in range(TPG):
                        last = pe.transpose(turned_sums[job % 2][:, t, 0:VC], acc_sb[job % 2][:, t * P:(t + 1) * P],
                                            W["ident"][0:VC, 0:VC])
                    last.then_inc(sums_ready, 1)

                def multiply(p, h, turned):
                    pair = PAIRS[p]
                    if p in (0, STEPS // BATCH):
                        pe.wait_ge(v_loaded[pair.e], 16 * (h + 1))
                    if pair.first:
                        pe.wait_ge(y_read, FREE_Y + h * JOBS + pair.job - 1)
                        pe.wait_ge(mrow_ready, turned)
                    pe.wait_ge(rest_dve, h * STEPS + p + 1)
                    pe.wait_ge(rest_pool, h * STEPS + p + 1)
                    high = prob[p % NP_BUF][:, :].bitcast(BF16)[:, 1::2]
                    for half, (kt, q0, at, _) in enumerate(pair.tiles):
                        v = vs[pair.e][:, kt, :]
                        pe.matmul(acc[pair.job % 2][0:VC, q0:GT], v, high[:, at:at + GT - q0],
                                  start=(pair.first and half == 0), stop=False)
                        last = pe.matmul(acc[pair.job % 2][0:VC, q0:GT], v, rest[p % NP_BUF][:, at:at + GT - q0],
                                         start=False, stop=pair.last and half == 1)
                    last.then_inc(pv_done, 1)

                def body(h, last):
                    turned = len(PRE_TURNS) + h * JOBS
                    for p in range(STEPS + 1):
                        chunks = share(p, last)
                        if p == STEPS - 1:
                            multiply(p, h, turned)
                        if chunks:
                            scores_q(chunks[0], h)
                        if p < STEPS and (k := pair_at(p + LAG, last)) is not None:
                            scores_k(k, h * STEPS + k, h)
                        for n in chunks[1:]:
                            scores_q(n, h)
                        if p < STEPS - 1:
                            multiply(p, h, turned)
                        if (job := ended(p - 1)) is not None:
                            turn_sums(job, h * JOBS + job)
                        for _, number in turns(p, h, last):
                            turn_maxima(number, h * JOBS + PAIRS[p].job, other_bank(p))
                            turned = turned + 1
                        if last and p == NEXT["y_turn"]:
                            pe.wait_ge(max_done, FREE_MAX + HEADS * NCH)
                            for c in range(KV):
                                F.y_turn(pe, 0, 0, c, s_max[c])
                        if last and p == NEXT["project"]:
                            F.project(pe, 0, s_max[0])
                        if last and p == NEXT["n_turn"]:
                            F.n_turn(pe, 0, s_max[1])
                        if last and p == NEXT["cut"]:
                            pe.wait_ge(F.cut_found, 1)
                            pe.matmul(s_max[0][0:1, 0:1], F.cut[:, :], W["ones"][:, :], start=True, stop=True)\
                              .then_inc(F.cut_counted, 1)
                        if last and p == NEXT["y_turn_1"]:
                            pe.wait_ge(F.cut_known, 1)
                            pe.wait_ge(F.xl_ready, 1)
                            for c in range(KV):
                                F.y_turn(pe, 0, 1, c, s_max[c])

                for n in range(LEAD + TURN):
                    if n < LEAD:
                        scores_q(n, 0)
                    if n >= TURN and ends_job(n - TURN):
                        turn_maxima(CHUNKS[n - TURN][0], 0, 1)
                for k in range(LAG):
                    scores_k(k, k, 0)
                heads(body)(pe)


def finish(nc, W, F, out):
    with ExitStack() as ctx:
        sb = lambda name, shape, dt: ctx.enter_context(nc.sbuf_tensor(name, shape, dt))
        sem = lambda name: ctx.enter_context(nc.semaphore("f_" + name))
        psum = lambda name, shape: ctx.enter_context(nc.psum_tensor(name, shape, F32))
        MT = HID // P
        two = range(2)
        xh, xl = F.xh, F.xl
        sg = [sb(f"f_sg{n}", [P, GT], F32) for n in two]
        full = sb("f_full", [P, MT, GT], F32)
        hi = [sb(f"f_hi{n}", [P, MT, GT], F32R) for n in two]
        lo = [sb(f"f_lo{n}", [P, MT, GT], F32R) for n in two]
        oT = sb("f_oT", [P, GT], F32)
        on = sb("f_on", [P, TPG, DM], F32)
        res = [sb(f"f_res{u}", [P, TPG, DM], F32) for u in two]
        ring = [psum(f"f_ring{n}", [P, GT]) for n in range(4)]
        psY = psum("f_psY", [P, GT])
        psO = psum("f_psO", [P, GT])
        psX = psum("f_psX", [P, GT])
        psN = psum("f_psN", [P, GT])
        y_banks = (psY, psO)

        yT_ready, nrm_ready, xh_ready, xl_ready = F.yT_ready, F.nrm_ready, F.xh_ready, F.xl_ready
        in_ready, silu_done, prod_done = sem("in_ready"), sem("silu_done"), sem("prod_done")
        hid_ready, gelu_done, hi_ready = sem("hid_ready"), sem("gelu_done"), sem("hi_ready")
        lo_dve, lo_pool = sem("lo_dve"), sem("lo_pool")
        o_ready, oT_ready, o_turned, on_ready = sem("o_ready"), sem("oT_ready"), sem("o_turned"), sem("on_ready")
        res_ready = sem("res_ready")
        stored = [sem(f"stored{u}") for u in two]
        HIGHS, LOWS_DVE, LOWS_POOL = 3 * MT, MT // 2 + 2 * MT, MT // 2

        def wait_low(eng, j, layer, m):
            if layer == 0 and m < MT // 2:
                eng.wait_ge(lo_pool, LOWS_POOL * j + m + 1)
            elif layer == 0:
                eng.wait_ge(lo_dve, 1 + LOWS_DVE * j + m - MT // 2 + 1)
            else:
                eng.wait_ge(lo_dve, 1 + LOWS_DVE * j + MT // 2 + (layer - 1) * MT + m + 1)

        def groups(eng, body):
            with eng.Fori(0, GROUPS // 2) as i:
                for u in two:
                    body(i, 2 * i + u, u)

        with nc.Block() as block:

            @block.sync
            def _(sp):
                for j in (2, 3):
                    sp.wait_ge(F.y_turned, KV * (j - 1))
                    F.load_y(sp, j, j % 2)

                def body(i, j, u):
                    sp.wait_ge(F.y_turned, KV * (j + 3))
                    F.load_y(sp, j + 4, u)
                    sp.wait_ge(res_ready, 1 + j + 1)
                    sp.dma_start(out[ds(j * GT, GT), :].rearrange("(t p) d -> p t d", p=P), res[1 - u][:, :, :])\
                      .then_inc(stored[1 - u], 16)
                groups(sp, body)
                for u in two:
                    sp.wait_ge(F.y_loaded[u], 16 * (2 + GROUPS // 2))
                sp.wait_ge(stored[0], 16 * (2 + GROUPS // 2))
                sp.wait_ge(stored[1], 16 * (1 + GROUPS // 2))

            @block.gpsimd
            def _(pool):
                pool.sem_inc(stored[0], 32)
                pool.sem_inc(stored[1], 16)

                def add_ffn(j, i, u):
                    pool.wait_ge(on_ready, j + 1)
                    pool.wait_ge(stored[u], 16 * (i + 1))
                    F.carry(pool)
                    pool.tensor_tensor(res[u][:, :, :], F.x_group(j + GROUPS - 1), on[:, :, :], ALU.add)\
                        .then_inc(res_ready, 1)

                def low(j, m):
                    pool.wait_ge(hi_ready, HIGHS * j + m + 1)
                    pool.tensor_tensor(lo[0][:, m, :], full[:, m, :], hi[0][:, m, :].bitcast(F32), ALU.subtract)\
                        .then_inc(lo_pool, 1)

                def body(i, j, u):
                    low(j, 0)
                    low(j, 1)
                    F.rstd_of(pool, "a", 1 + j + 1)
                    F.add_attention(pool, j + 1)
                    F.rstd_of(pool, "o", j + 1)
                    F.rstd_of(pool, "b", 1 + j + 1)
                    add_ffn(j, i, u)
                groups(pool, body)
                F.rstd_of(pool, "o", GROUPS + 1)
                add_ffn(GROUPS, GROUPS // 2, 0)

            @block.scalar
            def _(act):
                def o_out(j):
                    act.wait_ge(o_ready, j + 1)
                    act.wait_ge(o_turned, j + 1)
                    act.activation(oT[:, :], psN[:, :], ACT.Copy, scale=W["s3"][:, 0:1]).then_inc(oT_ready, 1)

                def body(i, j, u):
                    def high(m):
                        act.wait_ge(prod_done, MT * j + m + 1)
                        act.activation(hi[0][:, m, :], full[:, m, :], ACT.Copy).then_inc(hi_ready, 1)

                    for m in range(MT):
                        act.wait_ge(in_ready, 2 * (MT * j + m) + 1)
                        if m >= 2:
                            act.wait_ge(prod_done, MT * j + m - 1)
                        act.activation(sg[m % 2][:, :], ring[2 * m % 4][:, :], ACT.Silu, scale=W["s1"][:, m:m + 1])\
                           .then_inc(silu_done, 1)
                        if m >= 1:
                            high(m - 1)
                    high(MT - 1)
                    o_out(j)
                    for layer, scale in ((1, "sh1"), (2, "sh2")):
                        for m in range(MT):
                            act.wait_ge(hid_ready, 2 * MT * j + (layer - 1) * MT + m + 1)
                            s = W[scale][:, m:m + 1]
                            act.activation(hi[layer % 2][:, m, :], ring[m][:, :], ACT.Gelu, scale=s)\
                               .then_inc(hi_ready, 1)
                            wait_low(act, j, layer - 1, m)
                            act.activation(full[:, m, :], ring[m][:, :], ACT.Gelu, scale=s).then_inc(gelu_done, 1)
                            if layer == 2 and m == 2:
                                F.n_out(act, j + 1, psN)
                    F.y_out(act, j + 2, y_banks)
                groups(act, body)
                o_out(GROUPS)

            @block.vector
            def _(dve):
                dve.sem_inc(lo_dve, 1)
                dve.memset(psN[:, :], 0.0).then_inc(o_ready, 1)

                def output_moments(j):
                    dve.wait_ge(o_turned, 1 + j + 1)
                    F.moments(dve, "o", j + 1, lambda t: psO[:, t * P:(t + 1) * P])

                def output_normalise(j):
                    F.normalise(dve, "o", j + 1, on, lambda t: psO[:, t * P:(t + 1) * P], on_ready)

                def body(i, j, u):
                    def low(layer, m):
                        dve.wait_ge(hi_ready, HIGHS * j + layer * MT + m + 1)
                        if layer:
                            dve.wait_ge(gelu_done, 2 * MT * j + (layer - 1) * MT + m + 1)
                        dve.tensor_tensor(lo[layer % 2][:, m, :], full[:, m, :], hi[layer % 2][:, m, :].bitcast(F32),
                                          ALU.subtract).then_inc(lo_dve, 1)

                    dve.wait_ge(lo_dve, 1 + LOWS_DVE * j)
                    for m in range(MT):
                        dve.wait_ge(in_ready, 2 * (MT * j + m) + 2)
                        dve.wait_ge(silu_done, MT * j + m + 1)
                        dve.scalar_tensor_tensor(out=full[:, m, :], in0=ring[2 * m % 4 + 1][:, :],
                                                 scalar=W["s2"][:, m:m + 1], in1=sg[m % 2][:, :],
                                                 op0=ALU.mult, op1=ALU.mult).then_inc(prod_done, 1)
                    low(0, 2)
                    low(0, 3)
                    F.attention_moments(dve, j + 1, psX)
                    F.attention_normalise(dve, j + 1, psX)
                    low(1, 0)
                    output_moments(j)
                    low(1, 1)
                    low(1, 2)
                    F.x1_moments(dve, j + 1)
                    low(1, 3)
                    output_normalise(j)
                    F.x1_normalise(dve, j + 1)
                    low(2, 0)
                    low(2, 1)
                    low(2, 2)
                    F.n_low(dve, j + 1, psN)
                    low(2, 3)
                groups(dve, body)
                output_moments(GROUPS)
                output_normalise(GROUPS)

            @block.tensor
            def _(pe):
                pe.sem_inc(o_turned, 1)

                def o_turn(j):
                    pe.wait_ge(oT_ready, j + 1)
                    for t in range(TPG):
                        last = pe.transpose(psO[:, t * P:(t + 1) * P], oT[:, t * P:(t + 1) * P], W["ident"][:, :])
                    last.then_inc(o_turned, 1)

                def feed_forward(low_weights):
                    def product(bank, w, k, m, high, low, first, last):
                        at, _, outs = FFN_W[w]
                        at += k * outs + m * P
                        wh, wl = W["w_hi"][:, at:at + P], W["w_lo"][:, at:at + P]
                        pe.matmul(bank, wh, high, start=first, stop=False)
                        if low_weights:
                            pe.matmul(bank, wl, high, start=False, stop=False)
                        return pe.matmul(bank, wh, low, start=False, stop=last)

                    def hidden(w, layer, j, m, ks):
                        for k in ks:
                            if m == 0 or (m == 1 and k == MT - 1):
                                pe.wait_ge(hi_ready, HIGHS * j + (layer - 1) * MT + k + 1)
                                wait_low(pe, j, layer - 1, k)
                            last = product(ring[m][:, :], w, k, m, hi[(layer - 1) % 2][:, k, :],
                                           lo[(layer - 1) % 2][:, k, :], k == 0, k == MT - 1)
                        if ks[-1] == MT - 1:
                            last.then_inc(hid_ready, 1)

                    def body(i, j, u):
                        pe.wait_ge(xh_ready, j + 1)
                        pe.wait_ge(xl_ready, j + 1)
                        for m in range(MT):
                            if m == 2:
                                pe.wait_ge(nrm_ready, j + 1)
                                F.project(pe, j + 1, psX)
                            if m >= 2:
                                pe.wait_ge(prod_done, MT * j + m - 1)
                            for n, w in enumerate(("w1", "w2")):
                                product(ring[2 * m % 4 + n][:, :], w, 0, m, xh[:, :], xl[:, :], True, True)\
                                    .then_inc(in_ready, 1)
                        for layer, w in ((1, "h1"), (2, "h2")):
                            if layer == 1:
                                pe.wait_ge(prod_done, MT * j + MT - 1)
                            hidden(w, layer, j, 0, range(MT - 1))
                            hidden(w, layer, j, 1, range(MT - 1))
                            if layer == 1:
                                o_turn(j)
                            hidden(w, layer, j, 0, [MT - 1])
                            hidden(w, layer, j, 1, [MT - 1])
                            hidden(w, layer, j, 2, range(MT))
                            if layer == 2:
                                F.n_turn(pe, j + 1, psN)
                            hidden(w, layer, j, 3, range(MT))
                        pe.wait_ge(on_ready, j + 1)
                        for c in range(KV):
                            F.y_turn(pe, i + 1, u, c, y_banks[c])
                        pe.wait_ge(xl_ready, 1 + j + 1)
                        for k in range(MT):
                            pe.wait_ge(hi_ready, HIGHS * j + 2 * MT + k + 1)
                            wait_low(pe, j, 2, k)
                            last = product(psN[:, :], "w3", k, 0, hi[0][:, k, :], lo[0][:, k, :],
                                           k == 0, k == MT - 1)
                        last.then_inc(o_ready, 1)
                    groups(pe, body)

                any_low = pe.value_load(F.cut_count[0:1, 0:1], min_val=0, max_val=P)
                with pe.If(any_low == 0):
                    feed_forward(False)
                with pe.Else():
                    feed_forward(True)
                o_turn(GROUPS)


def kernel(L0_attn_x, L0_attn_wq, L0_attn_wk_down, L0_attn_wv_down, L0_attn_wk_up, L0_attn_wv_up, L0_attn_wo,
           L0_ffn_w1_w, L0_ffn_w1_s, L0_ffn_w2_w, L0_ffn_w2_s, L0_ffn_h1_w, L0_ffn_h1_s, L0_ffn_h2_w, L0_ffn_h2_s,
           L0_ffn_w3_w, L0_ffn_w3_s):
    import concourse.bacc as bacc
    from concourse.bass_utils import run_bass_kernel_spmd

    f = lambda a: np.ascontiguousarray(np.asarray(a))
    column = lambda s: f(np.asarray(s).reshape(-1, P).T)
    tiles = lambda w: np.asarray(w).T.reshape(-1, P, np.asarray(w).shape[0]).transpose(1, 0, 2).reshape(P, -1)
    ins = {
        "x": f(L0_attn_x).reshape(TOK, DM), "wqT": f(np.asarray(L0_attn_wq).T), "wkd": f(L0_attn_wk_down),
        "wvd": f(L0_attn_wv_down), "wkuT": f(np.asarray(L0_attn_wk_up).T), "wvuT": f(np.asarray(L0_attn_wv_up).T),
        "wo": f(L0_attn_wo), "ffn_w": np.concatenate([tiles(w) for w in (L0_ffn_w1_w, L0_ffn_w2_w, L0_ffn_h1_w,
                                                                  L0_ffn_h2_w, L0_ffn_w3_w)], axis=1), "s1": column(L0_ffn_w1_s), "s2": column(L0_ffn_w2_s),
        "sh1": column(L0_ffn_h1_s), "sh2": column(L0_ffn_h2_s), "s3": column(L0_ffn_w3_s),
    }
    nc = bacc.Bacc("TRN2", target_bir_lowering=False, num_devices=1)
    aps = {n: nc.dram_tensor("in_" + n, a.shape, F32, kind="ExternalInput").ap() for n, a in ins.items()}
    out = nc.dram_tensor("out_0", (TOK, DM), F32, kind="ExternalOutput").ap()
    layer(nc, *[aps[n] for n in ins], out)
    r = run_bass_kernel_spmd(nc, [{"in_" + n: a for n, a in ins.items()}], core_ids=[0])
    return r.results[0]["out_0"].reshape(BATCH, SEQ, DM)
```
